# Optimizing a Trainium2 kernel written in Bass

```python
import numpy as np
import jax
import jax.numpy as jnp

def _softmax(x, axis=-1):
    return jax.nn.softmax(x, axis=axis)

def _gelu(x):
    return jax.nn.gelu(x, approximate=True)

def _silu(x):
    return jax.nn.silu(x)

def _sigmoid(x):
    return jax.nn.sigmoid(x)

def _layernorm(x, axis=-1, eps=1e-05):
    m = jnp.mean(x, axis=axis, keepdims=True)
    v = jnp.var(x, axis=axis, keepdims=True)
    return (x - m) / jnp.sqrt(v + eps)

def _scatter_add(tgt, idx, src, axis=0):
    return tgt.at[idx].add(src)

def _segment_sum(src, seg, n):
    return jax.ops.segment_sum(src, seg, n)
kernel_name = 'mk_xattn_ffn_d2_seqx_r8_c124a0'

def setup_inputs(seed: int=0):
    np.random.seed(seed)
    _w = jnp.asarray

    def _rec_inputs():
        import jax
        import jax.numpy as jnp
        _rk = jax.random.key(seed)
        x = 7.22e-05 + 1 * jax.random.normal(jax.random.fold_in(_rk, 1), (16, 128, 256), jnp.float32)
        _lenS = 128 - jax.random.randint(jax.random.fold_in(_rk, 7), (16,), 0, max(1, 128 // 4) + 1, jnp.int32)
        _lenS2 = 128 - jax.random.randint(jax.random.fold_in(_rk, 8), (16,), 0, max(1, 128 // 4) + 1, jnp.int32)
        _ctx_512P = jax.random.normal(jax.random.fold_in(_rk, 11), (16, 16, 64), jnp.float32)
        _ctx_512c = jax.random.dirichlet(jax.random.fold_in(_rk, 511), 0.3 * jnp.ones((16,), jnp.float32), (16, 128))
        _ctx_512t = jnp.einsum('bsk,bkd->bsd', _ctx_512c, _ctx_512P)
        _ctx_512t = _ctx_512t * jax.lax.rsqrt(jnp.mean(jnp.square(_ctx_512t)) + 1e-12) * 0.953939
        ctx_512 = -0.000514642 + 1.00011 * (_ctx_512t + 0.3 * jax.random.normal(jax.random.fold_in(_rk, 611), (16, 128, 64), jnp.float32))
        return (x, ctx_512)
    x, ctx_512 = _rec_inputs()

    def _L0_xattn_setup():
        import jax, jax.numpy as jnp
        import numpy as np
        import math
        NUM_Q_HEADS = 32
        NUM_KV_HEADS = 8
        key = jax.random.key(seed)
        k1, k2, k3 = jax.random.split(key, 3)
        B, S, E = (2, 256, 256)
        kv_E = NUM_KV_HEADS * (E // NUM_Q_HEADS)
        q = jax.random.normal(k1, (B, S, E), dtype=jnp.float32)
        k = jax.random.normal(k2, (B, S, kv_E), dtype=jnp.float32)
        v = jax.random.normal(k3, (B, S, kv_E), dtype=jnp.float32)
        return {'q': q, 'k': k, 'v': v}
    _L0_xattn_all = _L0_xattn_setup()
    _L0_xattn_in = {k: v for k, v in _L0_xattn_all.items() if k in ()}
    del _L0_xattn_all

    def _L0_ffn_setup():
        import jax, jax.numpy as jnp
        import numpy as np
        DIM = 256
        HID = 128
        E = 8
        K = 2
        SHID = HID * 1
        INIT = 0.02
        key = jax.random.key(seed)
        ks = jax.random.split(key, 9)
        return {'x': jax.random.normal(ks[0], (2, 128, DIM), jnp.float32), 'expert_bias': jnp.zeros((E,), jnp.float32), 'gate_w': jax.random.normal(ks[1], (E, DIM), jnp.float32) * INIT, 'w1': jax.random.normal(ks[2], (E, HID, DIM), jnp.float32) * INIT, 'w2': jax.random.normal(ks[3], (E, DIM, HID), jnp.float32) * INIT, 'w3': jax.random.normal(ks[4], (E, HID, DIM), jnp.float32) * INIT, 'sw1': jax.random.normal(ks[5], (SHID, DIM), jnp.float32) * INIT, 'sw2': jax.random.normal(ks[6], (DIM, SHID), jnp.float32) * INIT, 'sw3': jax.random.normal(ks[7], (SHID, DIM), jnp.float32) * INIT}
    _L0_ffn_all = _L0_ffn_setup()
    _L0_ffn_in = {k: v for k, v in _L0_ffn_all.items() if k in ('expert_bias', 'gate_w', 'w1', 'w2', 'w3', 'sw1', 'sw2', 'sw3')}
    del _L0_ffn_all

    def _L1_xattn_setup():
        import jax, jax.numpy as jnp
        import numpy as np
        B, S, H, NH, L = (2, 256, 256, 16, 64)
        HD = H // NH
        key = jax.random.key(seed)
        k1, k2, k3, k4, k5 = jax.random.split(key, 5)
        scale = 0.02
        return {'q': jax.random.normal(k1, (B, S, H), dtype=jnp.float32), 'latent_kv': jax.random.normal(k2, (B, S, L), dtype=jnp.float32), 'Wq': jax.random.normal(k3, (H, H), dtype=jnp.float32) * scale, 'Wkv_expand': jax.random.normal(k4, (2 * H, L), dtype=jnp.float32) * scale, 'Wout': jax.random.normal(k5, (H, H), dtype=jnp.float32) * scale}
    _L1_xattn_all = _L1_xattn_setup()
    _L1_xattn_in = {k: v for k, v in _L1_xattn_all.items() if k in ('Wq', 'Wkv_expand', 'Wout')}
    del _L1_xattn_all

    def _L1_ffn_setup():
        import jax, jax.numpy as jnp
        import numpy as np
        import math
        GELU_C = math.sqrt(2.0 / math.pi)

        def activation_quant(x):
            scale = 127.0 / jnp.clip(jnp.max(jnp.abs(x), axis=-1, keepdims=True), 1e-05, None)
            y = jnp.clip(jnp.round(x * scale), -128, 127) / scale
            return x + jax.lax.stop_gradient(y - x)

        def weight_quant(w):
            scale = jnp.clip(jnp.mean(jnp.abs(w), axis=-1, keepdims=True), 1e-05, None)
            quant = jnp.clip(jnp.round(w / scale), -1, 1) * scale
            w_q = w + jax.lax.stop_gradient(quant - w)
            return (w_q / scale, scale.T)

        def new_gelu(x):
            return 0.5 * x * (1.0 + jnp.tanh(GELU_C * (x + 0.044715 * x * x * x)))

        def bitlinear(x, w):
            x_q = activation_quant(x)
            w_q, scale = weight_quant(w)
            out = jnp.einsum('bsd,hd->bsh', x_q, w_q)
            return out * scale
        key = jax.random.key(seed)
        k1, k2, k3 = jax.random.split(key, 3)
        dim, hidden = (256, 1024)
        B, S = (4, 256)
        x = jax.random.normal(k1, (B, S, dim), dtype=jnp.float32)
        lim1 = 1.0 / math.sqrt(dim)
        lim2 = 1.0 / math.sqrt(hidden)
        w1 = jax.random.uniform(k2, (hidden, dim), dtype=jnp.float32, minval=-lim1, maxval=lim1)
        w2 = jax.random.uniform(k3, (dim, hidden), dtype=jnp.float32, minval=-lim2, maxval=lim2)
        return {'x': x, 'w1': w1, 'w2': w2}
    _L1_ffn_all = _L1_ffn_setup()
    _L1_ffn_in = {k: v for k, v in _L1_ffn_all.items() if k in ('w1', 'w2')}
    del _L1_ffn_all
    return {'x': x, 'ctx_512': ctx_512, 'L0_ffn_expert_bias': _L0_ffn_in['expert_bias'], 'L0_ffn_gate_w': _L0_ffn_in['gate_w'], 'L0_ffn_w1': _L0_ffn_in['w1'], 'L0_ffn_w2': _L0_ffn_in['w2'], 'L0_ffn_w3': _L0_ffn_in['w3'], 'L0_ffn_sw1': _L0_ffn_in['sw1'], 'L0_ffn_sw2': _L0_ffn_in['sw2'], 'L0_ffn_sw3': _L0_ffn_in['sw3'], 'L1_xattn_Wq': _L1_xattn_in['Wq'], 'L1_xattn_Wkv_expand': _L1_xattn_in['Wkv_expand'], 'L1_xattn_Wout': _L1_xattn_in['Wout'], 'L1_ffn_w1': _L1_ffn_in['w1'], 'L1_ffn_w2': _L1_ffn_in['w2']}

def reference(x, ctx_512, L0_ffn_expert_bias, L0_ffn_gate_w, L0_ffn_w1, L0_ffn_w2, L0_ffn_w3, L0_ffn_sw1, L0_ffn_sw2, L0_ffn_sw3, L1_xattn_Wq, L1_xattn_Wkv_expand, L1_xattn_Wout, L1_ffn_w1, L1_ffn_w2):
    import jax
    import jax.numpy as jnp

    def _L0_xattn_ref(q, k, v):
        import jax, jax.numpy as jnp
        import numpy as np
        import math
        NUM_Q_HEADS = 32
        NUM_KV_HEADS = 8
        B, S, E = q.shape
        H, KV = (NUM_Q_HEADS, NUM_KV_HEADS)
        D = E // H
        G = H // KV
        scale = math.sqrt(D)
        qh = q.reshape(B, S, KV, G, D).transpose(0, 2, 3, 1, 4)
        kh = k.reshape(B, S, KV, D).transpose(0, 2, 1, 3)
        vh = v.reshape(B, S, KV, D).transpose(0, 2, 1, 3)
        scores = jnp.einsum('bkgsd,bktd->bkgst', qh, kh) / scale
        weights = jax.nn.softmax(scores, axis=-1)
        out = jnp.einsum('bkgst,bktd->bkgsd', weights, vh)
        return out.transpose(0, 3, 1, 2, 4).reshape(B, S, E)

    def _L0_ffn_ref(x, expert_bias, gate_w, w1, w2, w3, sw1, sw2, sw3):
        import jax, jax.numpy as jnp
        import numpy as np
        DIM = 256
        HID = 128
        E = 8
        K = 2
        SHID = HID * 1
        INIT = 0.02
        B, S, D = x.shape
        xf = x.reshape(-1, D)
        N = xf.shape[0]
        scores = jax.nn.sigmoid((xf @ gate_w.T).astype(jnp.float32))
        _, sel = jax.lax.top_k(scores + expert_bias[None, :], K)
        top_scores = jnp.take_along_axis(scores, sel, axis=1)
        flat_exp = sel.reshape(-1)
        order = jnp.argsort(flat_exp, stable=True)
        sorted_exp = flat_exp[order]
        tok_idx = order // K
        sc_sorted = top_scores.reshape(-1)[order]
        rin = xf[tok_idx] * sc_sorted[:, None].astype(x.dtype)
        out_sorted = jnp.zeros_like(rin)
        for e in range(E):
            m = (sorted_exp == e)[:, None].astype(rin.dtype)
            h = jax.nn.silu(rin @ w1[e].T) * (rin @ w3[e].T)
            out_sorted = out_sorted + m * (h @ w2[e].T)
        routed = jnp.zeros((N, D), x.dtype).at[tok_idx].add(out_sorted)
        shared = jax.nn.silu(xf @ sw1.T) * (xf @ sw3.T) @ sw2.T
        return (routed + shared).reshape(B, S, D)

    def _L1_xattn_ref(q, latent_kv, Wq, Wkv_expand, Wout):
        import jax, jax.numpy as jnp
        import numpy as np
        B, S, H, NH, L = (2, 256, 256, 16, 64)
        HD = H // NH
        b, sq, _ = q.shape
        sk = latent_kv.shape[1]
        qp = q @ Wq.T
        kv = latent_kv @ Wkv_expand.T
        k, v = jnp.split(kv, 2, axis=-1)
        qh = qp.reshape(b, sq, NH, HD).transpose(0, 2, 1, 3)
        kh = k.reshape(b, sk, NH, HD).transpose(0, 2, 1, 3)
        vh = v.reshape(b, sk, NH, HD).transpose(0, 2, 1, 3)
        inv_sqrt_d = 1.0 / jnp.sqrt(jnp.float32(HD))
        scores = jnp.einsum('bhqd,bhkd->bhqk', qh, kh) * inv_sqrt_d
        causal = jnp.tril(jnp.ones((sq, sk), dtype=bool))
        scores = jnp.where(causal, scores, jnp.finfo(scores.dtype).min)
        attn = jax.nn.softmax(scores, axis=-1)
        out = jnp.einsum('bhqk,bhkd->bhqd', attn, vh)
        out = out.transpose(0, 2, 1, 3).reshape(b, sq, H)
        return out @ Wout.T

    def _L1_ffn_ref(x, w1, w2):
        import jax, jax.numpy as jnp
        import numpy as np
        import math
        GELU_C = math.sqrt(2.0 / math.pi)

        def activation_quant(x):
            scale = 127.0 / jnp.clip(jnp.max(jnp.abs(x), axis=-1, keepdims=True), 1e-05, None)
            y = jnp.clip(jnp.round(x * scale), -128, 127) / scale
            return x + jax.lax.stop_gradient(y - x)

        def weight_quant(w):
            scale = jnp.clip(jnp.mean(jnp.abs(w), axis=-1, keepdims=True), 1e-05, None)
            quant = jnp.clip(jnp.round(w / scale), -1, 1) * scale
            w_q = w + jax.lax.stop_gradient(quant - w)
            return (w_q / scale, scale.T)

        def new_gelu(x):
            return 0.5 * x * (1.0 + jnp.tanh(GELU_C * (x + 0.044715 * x * x * x)))

        def bitlinear(x, w):
            x_q = activation_quant(x)
            w_q, scale = weight_quant(w)
            out = jnp.einsum('bsd,hd->bsh', x_q, w_q)
            return out * scale
        h = bitlinear(x, w1)
        h = new_gelu(h)
        return bitlinear(h, w2)
    x = x + _L0_xattn_ref(_layernorm(x, axis=-1), ctx_512, ctx_512)
    x = x + _L0_ffn_ref(_layernorm(x, axis=-1), L0_ffn_expert_bias, L0_ffn_gate_w, L0_ffn_w1, L0_ffn_w2, L0_ffn_w3, L0_ffn_sw1, L0_ffn_sw2, L0_ffn_sw3)
    x = x + _L1_xattn_ref(_layernorm(x, axis=-1), ctx_512, L1_xattn_Wq, L1_xattn_Wkv_expand, L1_xattn_Wout)
    x = x + _L1_ffn_ref(_layernorm(x, axis=-1), L1_ffn_w1, L1_ffn_w2)
    return x

_drawn_inputs = setup_inputs


def setup_inputs(seed=0):
    import zlib

    import numpy as np

    out = dict(_drawn_inputs(seed))
    spreads = {'L0_ffn_expert_bias': (0.0, 0.8)}
    factors = {'L0_ffn_gate_w': 8.0,
     'L0_ffn_w1': 8.0,
     'L0_ffn_w2': 8.0,
     'L0_ffn_w3': 8.0,
     'L0_ffn_sw1': 6.513,
     'L0_ffn_sw2': 6.416,
     'L0_ffn_sw3': 6.428,
     'L1_xattn_Wq': 29.023,
     'L1_xattn_Wkv_expand': 2.823,
     'L1_xattn_Wout': 2.909,
     'L1_ffn_w1': 4.123,
     'L1_ffn_w2': 3.992}
    for name, (base, spread) in spreads.items():
        noise = np.random.default_rng([zlib.crc32(name.encode()), seed]).standard_normal(out[name].shape)
        drawn = base * np.exp(spread * noise) if base else spread * noise
        out[name] = jnp.asarray(drawn.astype(out[name].dtype))
    for name, factor in factors.items():
        out[name] = (out[name] * factor).astype(out[name].dtype)
    return out
```

```python
from contextlib import ExitStack

import numpy as np

import concourse.bass as bass
from concourse import mybir

F32 = mybir.dt.float32
BF16 = mybir.dt.bfloat16
ALU = mybir.AluOpType
ACT = mybir.ActivationFunctionType
FREE = mybir.AxisListType.X

P = 128
D = 256
DC = D // P
L = 64
EPS = 1e-5
BANK = 512

KV0, G0, HD0 = 8, 4, 8
H0 = KV0 * G0
H1, HD1 = 16, 16
SLOT = 32
ONE0, ONE1 = HD0, HD1
NP = 6
K0, K1 = NP * HD0, NP * HD1
Q_PARTS = (slice(0, 3), slice(3, 5), slice(5, 6))
K_PARTS = (slice(1, 6, 2), slice(2, 5, 2), slice(0, 1))
KS = 96
KM = KS + 2

E, HID = 8, 128
NE = E + 1
HF = 1024
FC = HF // P

ROUND = 12582912.0
MASK = -3.0e38

SMALL_RING, BIG_RING = 4, 2

PARTS = {
    "A0": ([], []), "B0": ([], []), "C0": ([], []), "D0": ([], []),
    "AX": ([], []), "BX": ([], []), "CX": ([], []), "DX": ([], []),
    "A1": ([("KA_QA", 5, k) for k in range(1, 6)], []),
    "B1": ([("xTB", 1, 1)], []),
    "C1": ([("xTC", 1, 1)], []),
    "D1": ([("yT", 1, 1)], []),
    "C2": ([("qC_rest", 1, 1), ("kC_rest", 1, 1)], []),
    "B2": ([], [("vB", 3, 1)]),
    "A2": ([], [("nmA", 4, k) for k in range(1, 5)]),
    "D2": ([], [("z", 1, 1)]),
    "S": ([("f2_scale", 1, 1)], [("f1_scale", 1, 1)]),
    "C3": ([("KC_QC", 4, k) for k in range(1, 5)], []),
    "B3": ([], [("vB", 3, 2)]),
    "A3": ([("mTA", 1, 1)], []),
    "D2b": ([], []),
    "C4": ([], [("nmC", 2, k) for k in range(1, 3)]),
    "B4": ([], [("vB", 3, 3)]),
    "C5": ([("mTC", 1, 1)], []),
    "D2c": ([], []),
    "A4": ([], [("PA", 4, k) for k in range(1, 5)]),
    "B5": ([("hTB", 3, k) for k in range(1, 4)], []),
    "D3": ([("gT", 1, 1)], []),
    "C6": ([], [("PC", 2, k) for k in range(1, 3)]),
    "A5": ([("OA", 2, k) for k in range(1, 3)], []),
    "B6": ([("x2_done", 1, 1)], []),
    "C7": ([("OC", 1, 1)], []),
    "D4": ([("y2", 1, 1)], []),
    "A6": ([("oA", 2, k) for k in range(1, 3)], []),
    "C8": ([("oC", 1, 1)], []),
    "C9": ([("oTC", 1, 1)], []),
    "C10": ([("x3_done", 1, 1)], []),
}
STAGES = "ABCD"
SETUP_SLOT = 1
CHAIN = {
    "dve": {"A": 4, "B": 14, "C": 3, "D": 16, "S": 6},
    "pool": {"A": 6, "B": 0, "C": 4, "D": 0, "S": 0},
}


def stage_lag(part):
    return SETUP_SLOT if part == "S" else STAGES.index(part[0])


def active(part, n, tiles):
    return n == SETUP_SLOT if part == "S" else 0 <= n - stage_lag(part) < tiles


def ring_uses(slots, tiles, which, size):
    at, order = {}, []
    for n in range(slots):
        for part, rings in PARTS.items():
            if active(part, n, tiles):
                for j, release in enumerate(rings[which]):
                    before = order[len(order) - size] if len(order) >= size else None
                    at[n, part, j] = (len(order), before)
                    order.append((n, part, release))
    return at


def build(nc, a, out, TILES, looped=True):
    slots = TILES + len(STAGES) - 1
    first, step = len(STAGES) + 1, 2
    laps = (TILES - 2 - first) // step if looped else 0
    small_at = ring_uses(slots, TILES, 0, SMALL_RING)
    big_at = ring_uses(slots, TILES, 1, BIG_RING)
    lap_uses = [step * sum(len(r[w]) for p, r in PARTS.items() if p != "S") for w in range(2)]
    assert lap_uses[0] % SMALL_RING == 0 and lap_uses[1] % BIG_RING == 0

    with ExitStack() as ctx:
        def sb(name, shape, dt=F32):
            return ctx.enter_context(nc.sbuf_tensor(name, shape, dt))

        def sem(name):
            return ctx.enter_context(nc.semaphore(name))

        big = [ctx.enter_context(nc.psum_tensor(f"big{i}", [P, 2 * BANK], F32)) for i in range(BIG_RING)]
        small = [ctx.enter_context(nc.psum_tensor(f"small{i}", [P, BANK], F32)) for i in range(SMALL_RING)]
        big_full = [sem(f"big{i}_full") for i in range(BIG_RING)]
        small_full = [sem(f"small{i}_full") for i in range(SMALL_RING)]

        ident = sb("ident", [P, P])
        identb = sb("identb", [P, P], BF16)
        ones = sb("ones", [P, P])
        mask_st = sb("mask_st", [P, P], BF16)
        mask_ts = sb("mask_ts", [P, P], BF16)
        before = sb("before", [P, E, E])
        bias = sb("bias", [P, E])
        w_ab = [sb(f"w{n}T", [P, DC, E * HID]) for n in (1, 3)]
        w_sg = sb("sw1T_gateT", [P, DC, HID + E])
        w_s3 = sb("sw3T", [P, DC, HID])
        w_2 = sb("w2T", [P, NE, D])
        w_q = sb("WqT", [P, DC, D])
        w_kv = sb("WkvT", [L, 2 * D])
        w_o = sb("WoutT", [P, DC, D])
        f1 = sb("f1T", [P, DC, HF])
        f2 = sb("f2T", [P, FC, D])
        f1q = sb("f1q", [P, DC, HF], BF16)
        f2q = sb("f2q", [P, FC, D], BF16)
        f1s = sb("f1_scale", [P, HF])
        f2s = sb("f2_scale", [P, D])

        def two(name, shape, dt=F32):
            return [sb(f"{name}_{u}", shape, dt) for u in range(2)]

        x0, x1, x2, x3 = (two(f"x{i}", [P, D]) for i in range(4))
        x4 = two("x4", [P, D])
        cA = two("ctx", [P, L])
        cT = two("ctxT", [L, P])
        stats = {s: sb(f"stats{s}", [P, 6]) for s in STAGES}
        mv = {s: sb(f"mean_var{s}", [P, 2]) for s in STAGES}
        rstd = {s: sb(f"rstd{s}", [P, 1]) for s in STAGES}
        half = sb("minus_half", [P, 1])
        xn = {s: sb(f"xn{s}", [P, D]) for s in STAGES}
        qA = sb("qA", [P, H0, NP, HD0], BF16)
        qrA = sb("qrA", [P, D])
        kA = sb("kA", [P, KV0, NP, HD0], BF16)
        krA = sb("krA", [P, L])
        KA = sb("KA", [KM, KV0, P], BF16)
        QA = sb("QA", [KM, H0, P], BF16)
        nmA = sb("neg_maxA", [P, H0])
        nm2A = sb("neg_max2A", [P, 2, H0], BF16)
        mTA = sb("neg_maxT_A", [2 * H0, P], BF16)
        VA = two("VA", [P, KV0, SLOT])
        PA = sb("PA", [P, H0, P])
        OA = sb("OA", [P, 2, BANK])
        rlA = sb("rlA", [P, 2, H0 // 2])
        oA = sb("oA", [P, D])
        xTB = sb("xTB", [P, DC, P])
        eB = sb("gate_exp", [P, E])
        rt = {n: sb(f"route_{n}", [P, E]) for n in ("den", "score", "v", "rank", "sel", "half", "c")}
        gt = sb("gt", [P, E, E])
        eq = sb("eq", [P, E, E])
        tB = sb("tB", [P, NE * HID])
        uB = sb("uB", [P, NE * HID])
        vB = sb("vB", [P, NE * HID])
        hB = sb("hB", [P, NE * HID])
        hTB = sb("hTB", [P, NE, P])
        xTC = sb("xTC", [P, DC, P])
        qC = sb("qC", [P, H1, NP, HD1], BF16)
        kC = sb("kC", [P, H1, NP, HD1], BF16)
        qrC = sb("qrC", [P, D])
        krC = sb("krC", [P, D])
        KC = sb("KC", [KM, H1, P], BF16)
        QC = sb("QC", [KM, H1, P], BF16)
        nmC = sb("neg_maxC", [P, H1])
        nm2C = sb("neg_max2C", [P, 2, H1], BF16)
        mTC = sb("neg_maxT_C", [2 * H1, P], BF16)
        VC = sb("VC", [P, H1, SLOT])
        PC = sb("PC", [P, H1, P])
        OC = sb("OC", [P, BANK])
        rlC = sb("rlC", [P, H1])
        oC = sb("oC", [P, D])
        oTC = sb("oTC", [P, DC, P])
        am = sb("amax", [P, 4])
        qs1 = sb("qscale1", [P, 2])
        qs2 = sb("qscale2", [P, 2])
        yq = sb("yq", [P, D], BF16)
        yT = sb("yT", [P, DC, P], BF16)
        z = sb("z", [P, HF])
        zz = sb("zz", [P, HF])
        inner = sb("inner", [P, HF])
        th = sb("th", [P, HF])
        g2 = sb("g2", [P, HF])
        gq = sb("gq", [P, HF], BF16)
        gT = sb("gT", [P, FC, P], BF16)

        scratch = PA[:].rearrange("p h t -> p (h t)")
        f1a = scratch[:, 0:DC * HF].rearrange("p (c n) -> p c n", c=DC)
        f2a = scratch[:, DC * HF:].rearrange("p (k d) -> p k d", k=FC)
        wrec = g2

        w_in = {k: sem(f"w_in_{k}") for k in ("B", "C", "D1", "D2")}
        S = {k: sem(k) for k in (
            "consts", "idents", "stacks_set", "bias_in", "f1_abs", "f2_abs", "f1_scale", "f2_scale", "f1q", "f2q",
            "x_in0", "x_in1", "ctx_in0", "ctx_in1", "v_in0", "v_in1", "ctxT_in0", "ctxT_in1", "stored0", "stored1",
            "varA", "varB", "varC", "varD", "rstdA", "rstdB", "rstdC", "rstdD", "xnA", "xnB", "xnC",
            "kA_hi", "qA_hi", "kA", "qA", "KA_QA", "nmA", "nm2A", "mTA", "mrowsA", "PA", "OA", "rlA", "oA", "x1_done",
            "xTB", "gate_exp", "score", "route_c", "tB", "vB", "hB", "hTB", "x2_done",
            "xTC", "qC_hi", "kC_hi", "VC", "qC_rest", "kC_rest", "qC", "kC", "KC_QC", "nmC", "nm2C", "mTC", "mrowsC",
            "PC", "OC", "rlC", "oC", "oTC", "x3_done",
            "yq", "yT", "z", "zz", "inner", "th", "gq", "gT", "y2", "x4_done")}
        chain_sem = {(e, s): sem(f"{e}_step_{s}") for e in CHAIN for s in CHAIN[e]}

        pool_fill, dve_set, settled = sem("pool_fill"), sem("dve_set"), sem("settled")

        class Slot:

            def __init__(self, eng, n, lap=None):
                self.eng, self.n, self.lap = eng, n, lap

            def at(self, base, per_lap):
                return base if self.lap is None else base + self.lap * per_lap

            def tile(self, part):
                return self.at(self.n - stage_lag(part), step)

            def wait(self, name, t, per_tile=1, k=None):
                self.eng.wait_ge(S[name], t * per_tile + (per_tile if k is None else k))

            def settle(self):
                self.eng.sem_inc(settled, 1)

            def before(self, name, t, per_tile=1):
                if not (isinstance(t, int) and t == 0):
                    self.eng.wait_ge(S[name], t * per_tile)

            def _fill(self, part, j, at, which, ring, full):
                use, prior = at[self.n, part, j]
                if prior is not None:
                    n, p, (name, per_tile, k) = prior
                    self.eng.wait_ge(S[name], self.at((n - stage_lag(p)) * per_tile + k, step * per_tile))
                return ring[use % len(ring)], full[use % len(ring)]

            def _read(self, part, j, at, which, ring, full):
                use = at[self.n, part, j][0]
                size = len(ring)
                self.eng.wait_ge(full[use % size], self.at(use // size + 1, lap_uses[which] // size))
                return ring[use % size]

            def fill_small(self, part, j=0):
                return self._fill(part, j, small_at, 0, small, small_full)

            def fill_big(self, part, j=0):
                return self._fill(part, j, big_at, 1, big, big_full)

            def read_small(self, part, j=0):
                return self._read(part, j, small_at, 0, small, small_full)

            def read_big(self, part, j=0):
                return self._read(part, j, big_at, 1, big, big_full)

        class Chain:

            def __init__(self, eng, kind):
                self.eng, self.per, self.kind = eng, CHAIN[kind], kind
                self.done = dict.fromkeys(self.per, 0)

            def __call__(self, stage, t, ins, wait=True):
                ins.then_inc(chain_sem[self.kind, stage], 1)
                self.done[stage] += 1
                if wait:
                    self.eng.wait_ge(chain_sem[self.kind, stage], t * self.per[stage] + self.done[stage])

            def end_slot(self):
                for s, k in self.done.items():
                    assert k in (0, self.per[s]), (self.kind, s, k)
                    self.done[s] = 0

        def walk(eng, parts, chain=None):
            def emit(n, lap=None):
                slot = Slot(eng, n, lap)
                for part in PARTS:
                    if active(part, n, TILES) and part in parts:
                        u = (n - stage_lag(part)) % 2
                        parts[part](slot, 0 if part == "S" else slot.tile(part), u)
                if chain:
                    chain.end_slot()

            n = 0
            while n < slots:
                if laps and n == first:
                    with eng.Fori(0, laps) as lap:
                        for i in range(step):
                            emit(first + i, lap)
                    n += laps * step
                else:
                    emit(n)
                    n += 1

        def wait_in(eng, name, t, u):
            eng.wait_ge(S[f"{name}{u}"], (t + (2 - u)) * 8)

        block = ctx.enter_context(nc.Block())

        @block.sync
        def _(sp):
            def load(u, t):
                sp.dma_start(x0[u][:], a["x"][t]).then_inc(S[f"x_in{u}"], 16)
                sp.dma_start(cA[u][:], a["ctx"][t]).then_inc(S[f"ctx_in{u}"], 16)
                sp.dma_start(VA[u][:, :, 0:HD0], a["ctx"][t].rearrange("p (h d) -> p h d", d=HD0)).then_inc(S[f"v_in{u}"], 16)

            def S_load():
                sp.dma_start(bias[:], a["bias"].unsqueeze(0).broadcast_to([P, E])).then_inc(S["bias_in"], 16)
                for c in range(DC):
                    sp.dma_start(w_sg[:, c, 0:HID], a["sw1T"][c]).then_inc(w_in["B"], 16)
                    sp.dma_start(w_sg[:, c, HID:HID + E], a["gateT"][c]).then_inc(w_in["B"], 16)
                    sp.dma_start(w_s3[:, c, :], a["sw3T"][c]).then_inc(w_in["B"], 16)
                    sp.dma_start(w_ab[0][:, c, :], a["w1T"][c]).then_inc(w_in["B"], 16)
                    sp.dma_start(w_ab[1][:, c, :], a["w3T"][c]).then_inc(w_in["B"], 16)
                sp.dma_start(w_2[:, 0:E, :], a["w2T"].rearrange("e h d -> h e d")).then_inc(w_in["B"], 16)
                sp.dma_start(w_2[:, E, :], a["sw2T"]).then_inc(w_in["B"], 16)
                for c in range(DC):
                    sp.dma_start(f1[:, c, :], a["f1T"][c]).then_inc(w_in["D1"], 16)
                sp.dma_start(f2[:], a["f2T"].rearrange("k p d -> p k d")).then_inc(w_in["D2"], 16)
                for c in range(DC):
                    sp.dma_start(w_q[:, c, :], a["WqT"][c]).then_inc(w_in["C"], 16)
                    sp.dma_start(w_o[:, c, :], a["WoutT"][c]).then_inc(w_in["C"], 16)
                sp.dma_start(w_kv[:], a["WkvT"]).then_inc(w_in["C"], 16)

            sp.wait_ge(S["consts"], 1)
            load(0, 0)
            S_load()
            load(1, 1)

            def A3(s, t, u):
                s.wait("mTA", t)
                for i in range(2):
                    sp.dma_start(QA[KS + i:KS + i + 1, :, :], mTA[i * H0:(i + 1) * H0, :]).then_inc(S["mrowsA"], 16)

            def C5(s, t, u):
                s.wait("mTC", t)
                for i in range(2):
                    sp.dma_start(QC[KS + i:KS + i + 1, :, :], mTC[i * H1:(i + 1) * H1, :]).then_inc(S["mrowsC"], 16)

            def C0(s, t, u):
                s.before("VC", t)
                sp.dma_start(cT[u][:], a["ctxT"][t]).then_inc(S[f"ctxT_in{u}"], 16)

            def A6(s, t, u):
                if isinstance(t, int) and t + 2 >= TILES:
                    return
                s.wait("x1_done", t)
                load(u, t + 2)

            def D4(s, t, u):
                s.wait("x4_done", t)
                sp.dma_start(out[t], x4[u][:]).then_inc(S[f"stored{u}"], 16)

            walk(sp, {"A3": A3, "C0": C0, "C5": C5, "A6": A6, "D4": D4})
            for u in range(2):
                sp.wait_ge(S[f"stored{u}"], 16 * (TILES // 2))

        @block.tensor
        def _(pe):
            mm, transpose = nc.tensor.matmul, nc.tensor.transpose

            def bf(ps):
                return ps[:].bitcast(BF16)

            def heads_of(ps):
                return bf(ps).rearrange("p (h t) -> p h t", t=P)

            def S_(s, t, u):
                s.eng.wait_ge(S["f1_abs"], 1)
                ps, full = s.fill_big("S")
                for b in range(2):
                    for c in range(DC):
                        last = mm(ps[:, b * BANK:(b + 1) * BANK], ones[:], f1a[:, c, b * BANK:(b + 1) * BANK],
                                  start=(c == 0), stop=(c == DC - 1))
                last.then_inc(full, 1)
                s.eng.wait_ge(S["f2_abs"], 1)
                ps, full = s.fill_small("S")
                for k in range(FC):
                    last = mm(ps[:, 0:D], ones[:], f2a[:, k, :], start=(k == 0), stop=(k == FC - 1))
                last.then_inc(full, 1)

            def stack(s, part, j, src, h0, rows):
                ps, full = s.fill_small(part, j)
                s.settle()
                for i in range(8):
                    last = transpose(heads_of(ps)[0:rows, i, :], src[:, h0 + i, :, :].rearrange("p i d -> p (i d)"), identb[:])
                last.then_inc(full, 1)

            def A1(s, t, u):
                s.wait("kA", t)
                stack(s, "A1", 0, kA, 0, K0)
                s.wait("qA", t)
                for j in range(4):
                    stack(s, "A1", 1 + j, qA, 8 * j, K0)

            def A2(s, t, u):
                for j in range(4):
                    s.wait("KA_QA", t, 5, j + 2)
                    ps, full = s.fill_big("A2", j)
                    for i in range(8):
                        h = 8 * j + i
                        last = mm(ps[:, i * P:(i + 1) * P], QA[0:KS, h, :], KA[0:KS, h // G0, :], start=True, stop=True)
                    last.then_inc(full, 1)

            def A3(s, t, u):
                s.wait("nm2A", t)
                ps, full = s.fill_small("A3")
                s.settle()
                transpose(bf(ps)[0:2 * H0, 0:P], nm2A[:].rearrange("p i h -> p (i h)"), identb[:]).then_inc(full, 1)

            def A4(s, t, u):
                s.wait("mrowsA", t, 32)
                for j in range(4):
                    ps, full = s.fill_big("A4", j)
                    for i in range(2):
                        kv = 2 * j + i
                        last = mm(ps[:, i * BANK:(i + 1) * BANK], KA[:, kv, :], QA[:, kv * G0:(kv + 1) * G0, :],
                                  start=True, stop=True)
                    last.then_inc(full, 1)

            def A5(s, t, u):
                wait_in(pe, "v_in", t, u)
                for r in range(2):
                    s.wait("PA", t, 4, 2 * r + 2)
                    ps, full = s.fill_small("A5", r)
                    for j in range(4):
                        kv = 4 * r + j
                        last = mm(ps[SLOT * j:SLOT * (j + 1), :], VA[u][:, kv, :], PA[:, kv * G0:(kv + 1) * G0, :],
                                  start=True, stop=True)
                    last.then_inc(full, 1)

            def A6(s, t, u):
                for r in range(2):
                    s.wait("OA", t, 2, r + 1)
                    ps, full = s.fill_small("A6", r)
                    for g in range(G0):
                        last = transpose(ps[:, g * P:(g + 1) * P], OA[:, r, g * P:(g + 1) * P], ident[:])
                    last.then_inc(full, 1)

            def turn(s, part, src, idn):
                ps, full = s.fill_small(part)
                dst = ps if src.dtype == F32 else bf(ps)
                for c in range(DC):
                    last = transpose(dst[:, c * P:(c + 1) * P], src[:, c * P:(c + 1) * P], idn[:])
                last.then_inc(full, 1)

            def B1(s, t, u):
                s.wait("xnB", t)
                turn(s, "B1", xn["B"], ident)

            def experts(s, part, wa, wb, na, nb):
                ps, full = s.fill_big(part)
                for w, n, o in ((wa, na, 0), (wb, nb, BANK)):
                    for c in range(DC):
                        last = mm(ps[:, o:o + n], xTB[:, c, :], w[c], start=(c == 0), stop=(c == DC - 1))
                last.then_inc(full, 1)

            def B2(s, t, u):
                if isinstance(t, int) and t == 0:
                    pe.wait_ge(w_in["B"], 16 * (5 * DC + 2))
                s.wait("xTB", t)
                experts(s, "B2", [w_sg[:, c, :] for c in range(DC)], [w_s3[:, c, :] for c in range(DC)], HID + E, HID)

            def B3(s, t, u):
                experts(s, "B3", *([w[:, c, 0:BANK] for c in range(DC)] for w in w_ab), BANK, BANK)

            def B4(s, t, u):
                experts(s, "B4", *([w[:, c, BANK:] for c in range(DC)] for w in w_ab), BANK, BANK)

            def B5(s, t, u):
                for j, (e0, n) in enumerate(((8, 1), (0, 4), (4, 4))):
                    if j == 0:
                        s.wait("vB", t, 3, 1)
                    else:
                        s.wait("hB", t, 2, j)
                    ps, full = s.fill_small("B5", j)
                    for i in range(n):
                        last = transpose(ps[:, i * P:(i + 1) * P], hB[:, (e0 + i) * HID:(e0 + i + 1) * HID], ident[:])
                    last.then_inc(full, 1)

            def B6(s, t, u):
                s.wait("hTB", t, 3)
                ps, full = s.fill_small("B6")
                for e in range(NE):
                    last = mm(ps[:, 0:D], hTB[:, e, :], w_2[:, e, :], start=(e == 0), stop=(e == NE - 1))
                last.then_inc(full, 1)

            def C1(s, t, u):
                s.wait("xnC", t)
                turn(s, "C1", xn["C"], ident)

            def C2(s, t, u):
                if isinstance(t, int) and t == 0:
                    pe.wait_ge(w_in["C"], 16 * (2 * DC + 1))
                s.wait("xTC", t)
                ps, full = s.fill_small("C2", 0)
                for c in range(DC):
                    last = mm(ps[:, 0:D], xTC[:, c, :], w_q[:, c, :], start=(c == 0), stop=(c == DC - 1))
                last.then_inc(full, 1)
                wait_in(pe, "ctxT_in", t, u)
                ps, full = s.fill_small("C2", 1)
                mm(ps[:], cT[u][:], w_kv[:], start=True, stop=True).then_inc(full, 1)

            def C3(s, t, u):
                for j in range(4):
                    s.wait(("qC", "kC")[j // 2], t)
                    stack(s, "C3", j, (qC, kC)[j // 2], 8 * (j % 2), K1)

            def causal(s, part, mask, rows, lhs, rhs):
                for j in range(2):
                    ps, full = s.fill_big(part, j)
                    for b in range(2):
                        mm(ps[:, b * BANK:(b + 1) * BANK], identb[:], mask[:].unsqueeze(1).broadcast_to([P, 4, P]),
                           start=True, stop=False)
                        for i in range(4):
                            h = 8 * j + 4 * b + i
                            last = mm(ps[:, b * BANK + i * P:b * BANK + (i + 1) * P], lhs[0:rows, h, :], rhs[0:rows, h, :],
                                      start=False, stop=(i == 3))
                    last.then_inc(full, 1)

            def C4(s, t, u):
                s.wait("KC_QC", t, 4)
                causal(s, "C4", mask_st, KS, QC, KC)

            def C5(s, t, u):
                s.wait("nm2C", t)
                ps, full = s.fill_small("C5")
                transpose(bf(ps)[0:2 * H1, 0:P], nm2C[:].rearrange("p i h -> p (i h)"), identb[:]).then_inc(full, 1)

            def C6(s, t, u):
                s.wait("mrowsC", t, 32)
                causal(s, "C6", mask_ts, KM, KC, QC)

            def C7(s, t, u):
                s.wait("PC", t, 2)
                ps, full = s.fill_small("C7")
                for i in range(4):
                    for j in range(4):
                        h = 4 * i + j
                        last = mm(ps[SLOT * j:SLOT * (j + 1), i * P:(i + 1) * P], VC[:, h, :], PC[:, h, :],
                                  start=True, stop=True)
                last.then_inc(full, 1)

            def C8(s, t, u):
                s.wait("OC", t)
                ps, full = s.fill_small("C8")
                for i in range(4):
                    last = transpose(ps[:, i * P:(i + 1) * P], OC[:, i * P:(i + 1) * P], ident[:])
                last.then_inc(full, 1)

            def C9(s, t, u):
                s.wait("oC", t)
                turn(s, "C9", oC, ident)

            def C10(s, t, u):
                s.wait("oTC", t)
                ps, full = s.fill_small("C10")
                for c in range(DC):
                    last = mm(ps[:, 0:D], oTC[:, c, :], w_o[:, c, :], start=(c == 0), stop=(c == DC - 1))
                last.then_inc(full, 1)

            def D1(s, t, u):
                s.wait("yq", t)
                turn(s, "D1", yq, identb)

            def D2(s, t, u):
                if isinstance(t, int) and t == 0:
                    pe.wait_ge(S["f1q"], 1)
                s.wait("yT", t)
                ps, full = s.fill_big("D2")
                for b in range(2):
                    for c in range(DC):
                        last = mm(ps[:, b * BANK:(b + 1) * BANK], yT[:, c, :], f1q[:, c, b * BANK:(b + 1) * BANK],
                                  start=(c == 0), stop=(c == DC - 1))
                last.then_inc(full, 1)

            def D3(s, t, u):
                s.wait("gq", t)
                ps, full = s.fill_small("D3")
                for k in range(FC):
                    last = transpose(bf(ps)[:, k * P:(k + 1) * P], gq[:, k * P:(k + 1) * P], identb[:])
                last.then_inc(full, 1)

            def D4(s, t, u):
                if isinstance(t, int) and t == 0:
                    pe.wait_ge(S["f2q"], 1)
                s.wait("gT", t)
                ps, full = s.fill_small("D4")
                for k in range(FC):
                    last = mm(ps[:, 0:D], gT[:, k, :], f2q[:, k, :], start=(k == 0), stop=(k == FC - 1))
                last.then_inc(full, 1)

            pe.wait_ge(S["idents"], 1)
            pe.wait_ge(S["consts"], 2)
            walk(pe, {"S": S_, "A1": A1, "A2": A2, "A3": A3, "A4": A4, "A5": A5, "A6": A6, "B1": B1, "B2": B2, "B3": B3,
                      "B4": B4, "B5": B5, "B6": B6, "C1": C1, "C2": C2, "C3": C3, "C4": C4, "C5": C5, "C6": C6, "C7": C7,
                      "C8": C8, "C9": C9, "C10": C10, "D1": D1, "D2": D2, "D3": D3, "D4": D4})

        @block.scalar
        def _(act):
            op = nc.scalar.activation

            def S_(s, t, u):
                act.wait_ge(w_in["D1"], 16 * DC)
                op(f1a, f1[:], ACT.Abs).then_inc(S["f1_abs"], 1)
                act.wait_ge(w_in["D2"], 16)
                op(f2a, f2[:], ACT.Abs).then_inc(S["f2_abs"], 1)

            def A3(s, t, u):
                ps = s.read_small("A3")
                s.before("mrowsA", t, 32)
                op(mTA[:], ps[:].bitcast(BF16)[0:2 * H0, 0:P], ACT.Copy).then_inc(S["mTA"], 1)

            def C5(s, t, u):
                ps = s.read_small("C5")
                s.before("mrowsC", t, 32)
                op(mTC[:], ps[:].bitcast(BF16)[0:2 * H1, 0:P], ACT.Copy).then_inc(S["mTC"], 1)

            def exps(s, part, n, dst, scale, name):
                for j in range(n):
                    ps = s.read_big(part, j)
                    op(dst[:, 8 * j:8 * (j + 1), :], ps[:].rearrange("p (h t) -> p h t", t=P), ACT.Exp,
                       scale=scale).then_inc(S[name], 1)

            def A4(s, t, u):
                exps(s, "A4", 4, PA, float(HD0) ** -0.5, "PA")

            def A5(s, t, u):
                for r in range(2):
                    ps = s.read_small("A5", r)
                    s.before("oA", t, 2)
                    op(OA[:, r, :], ps[:], ACT.Copy).then_inc(S["OA"], 1)

            def B1(s, t, u):
                ps = s.read_small("B1")
                op(xTB[:].rearrange("p c t -> p (c t)"), ps[:, 0:D], ACT.Copy).then_inc(S["xTB"], 1)

            def B2(s, t, u):
                ps = s.read_big("B2")
                op(eB[:], ps[:, HID:HID + E], ACT.Exp, scale=-1.0).then_inc(S["gate_exp"], 1)
                s.before("vB", t, 3)
                op(tB[:, E * HID:], ps[:, 0:HID], ACT.Tanh, scale=0.5).then_inc(S["tB"], 1)

            def silu_tanh(s, part, t, e0):
                ps = s.read_big(part)
                s.wait("score", t)
                for i in range(4):
                    ins = op(tB[:, (e0 + i) * HID:(e0 + i + 1) * HID], ps[:, i * HID:(i + 1) * HID], ACT.Tanh,
                             scale=rt["half"][:, e0 + i:e0 + i + 1])
                ins.then_inc(S["tB"], 1)

            def B3(s, t, u):
                silu_tanh(s, "B3", t, 0)

            def B4(s, t, u):
                silu_tanh(s, "B4", t, 4)

            def B5(s, t, u):
                s.before("x2_done", t)
                for j, (e0, n) in enumerate(((8, 1), (0, 4), (4, 4))):
                    ps = s.read_small("B5", j)
                    op(hTB[:, e0:e0 + n, :], ps[:, 0:n * P].rearrange("p (e t) -> p e t", t=P), ACT.Copy)\
                        .then_inc(S["hTB"], 1)

            def C1(s, t, u):
                ps = s.read_small("C1")
                op(xTC[:].rearrange("p c t -> p (c t)"), ps[:, 0:D], ACT.Copy).then_inc(S["xTC"], 1)

            def high(dst, where, src, heads):
                n = len(range(NP)[where])
                src = src.rearrange("p (h d) -> p h d", h=heads).unsqueeze(2)
                shape = [P, heads, n, src.shape[3]]
                return op(dst[:, :, where, :], src.broadcast_to(shape), ACT.Copy)

            def AX(s, t, u):
                s.before("KA_QA", t, 5)
                wait_in(act, "ctx_in", t, u)
                high(kA, K_PARTS[0], cA[u][:], KV0).then_inc(S["kA_hi"], 1)
                s.wait("xnA", t)
                high(qA, Q_PARTS[0], xn["A"][:], H0).then_inc(S["qA_hi"], 1)

            def C2(s, t, u):
                ps = s.read_small("C2", 0)
                s.before("KC_QC", t, 4)
                high(qC, Q_PARTS[0], ps[:, 0:D], H1).then_inc(S["qC_hi"], 1)
                ps = s.read_small("C2", 1)
                high(kC, K_PARTS[0], ps[:, 0:D], H1).then_inc(S["kC_hi"], 1)
                op(VC[:, :, 0:HD1], ps[:, D:2 * D].rearrange("p (h d) -> p h d", d=HD1), ACT.Copy).then_inc(S["VC"], 1)

            def C3(s, t, u):
                for j in range(4):
                    ps = s.read_small("C3", j)
                    op((QC, KC)[j // 2][0:K1, 8 * (j % 2):8 * (j % 2) + 8, :],
                       ps[:].bitcast(BF16).rearrange("p (h t) -> p h t", t=P)[0:K1], ACT.Copy).then_inc(S["KC_QC"], 1)

            def C6(s, t, u):
                exps(s, "C6", 2, PC, float(HD1) ** -0.5, "PC")

            def C7(s, t, u):
                ps = s.read_small("C7")
                s.before("oC", t)
                op(OC[:], ps[:], ACT.Copy).then_inc(S["OC"], 1)

            def C9(s, t, u):
                ps = s.read_small("C9")
                op(oTC[:].rearrange("p c t -> p (c t)"), ps[:, 0:D], ACT.Copy).then_inc(S["oTC"], 1)

            def D2(s, t, u):
                s.wait("z", t)
                op(zz[:], z[:], ACT.Square, scale=0.044715 ** 0.5).then_inc(S["zz"], 1)

            def D2b(s, t, u):
                s.wait("inner", t)
                op(th[:], inner[:], ACT.Tanh, scale=(2.0 / np.pi) ** 0.5).then_inc(S["th"], 1)

            act.wait_ge(S["stacks_set"], 1)
            walk(act, {"S": S_, "AX": AX, "A3": A3, "A4": A4, "A5": A5, "B1": B1, "B2": B2, "B3": B3, "B4": B4, "B5": B5, "C1": C1,
                       "C2": C2, "C3": C3, "C5": C5, "C6": C6, "C7": C7, "C9": C9, "D2": D2, "D2b": D2b})

        @block.gpsimd
        def _(pool):
            g = nc.gpsimd
            fills = [0]

            def filled(ins):
                fills[0] += 1
                ins.then_inc(pool_fill, 1)

            def after_fills():
                pool.wait_ge(pool_fill, fills[0])

            for v in VA:
                filled(g.memset(v[:, :, HD0:SLOT], 0.0))
            filled(g.memset(half[:], -0.5))
            filled(g.memset(ident[:], 0.0))
            after_fills()
            filled(g.affine_select(out=ident[:], in_=ident[:], compare_op=ALU.not_equal, fill=1.0, base=0,
                                   pattern=[[-1, P]], channel_multiplier=1))
            for v in VA:
                filled(g.memset(v[:, :, ONE0:ONE0 + 1], 1.0))
            after_fills()
            g.memset(VC[:], 0.0).then_inc(S["consts"], 1)
            filled(g.memset(mask_st[:], 0.0))
            filled(g.memset(mask_ts[:], 0.0))
            filled(g.memset(before[:], 0.0))
            pool.wait_ge(S["consts"], 1)
            after_fills()
            filled(g.memset(VC[:, :, ONE1:ONE1 + 1], 1.0))
            filled(g.affine_select(out=mask_st[:], in_=mask_st[:], compare_op=ALU.is_ge, fill=MASK, base=0,
                                   pattern=[[-1, P]], channel_multiplier=1))
            filled(g.affine_select(out=mask_ts[:], in_=mask_ts[:], compare_op=ALU.is_ge, fill=MASK, base=0,
                                   pattern=[[1, P]], channel_multiplier=-1))
            g.affine_select(out=before[:], in_=before[:], compare_op=ALU.is_ge, fill=1.0, base=0,
                            pattern=[[-1, E], [1, E]], channel_multiplier=0).then_inc(S["consts"], 1)
            after_fills()

            chain = Chain(pool, "pool")

            def inv_std(stage):
                def part(s, t, u):
                    s.wait(f"var{stage}", t)
                    g.tensor_tensor(rstd[stage][:], mv[stage][:, 1:2], half[:], ALU.pow).then_inc(S[f"rstd{stage}"], 1)
                return part

            def lower(s, stage, t, dst, where, rest, heads, name):
                rest = rest[:].rearrange("p (h d) -> p h d", h=heads)
                mid, low = dst[:, :, where[1], :], dst[:, :, where[2], :]
                s.settle()
                for i in range(2):
                    chain(stage, t, g.tensor_copy(mid[:, :, i, :], rest), wait=(i == 1))
                g.tensor_tensor(low[:, :, 0, :], rest, mid[:, :, 0, :], ALU.subtract).then_inc(S[name], 1)

            def AX(s, t, u):
                s.before("KA_QA", t, 5)
                for x, name, dst, where, rest, heads in ((cA[u], "kA", kA, K_PARTS, krA, KV0),
                                                         (xn["A"], "qA", qA, Q_PARTS, qrA, H0)):
                    s.wait(f"{name}_hi", t)
                    high = dst[:, :, where[0], :][:, :, 0, :]
                    chain("A", t, g.tensor_tensor(rest[:].rearrange("p (h d) -> p h d", h=heads),
                                                  x[:].rearrange("p (h d) -> p h d", h=heads), high, ALU.subtract))
                    lower(s, "A", t, dst, where, rest, heads, name)

            def B3(s, t, u):
                s.wait("route_c", t)
                s.before("hTB", t, 3)
                weigh(s, t, 0, 2, 1)

            def B4(s, t, u):
                weigh(s, t, 4, 3, 2)

            def weigh(s, t, e0, k, done):
                s.wait("vB", t, 3, k)
                sl = slice(e0 * HID, (e0 + 4) * HID)
                g.tensor_tensor(hB[:, sl].rearrange("p (e h) -> p e h", e=4), vB[:, sl].rearrange("p (e h) -> p e h", e=4),
                                rt["c"][:, e0:e0 + 4].unsqueeze(2).broadcast_to([P, 4, HID]), ALU.mult)\
                    .then_inc(S["hB"], 1)

            def C2(s, t, u):
                s.wait("qC_rest", t)
                lower(s, "C", t, qC, Q_PARTS, qrC, H1, "qC")
                s.wait("kC_rest", t)
                lower(s, "C", t, kC, K_PARTS, krC, H1, "kC")

            walk(pool, {"A0": inv_std("A"), "B0": inv_std("B"), "C0": inv_std("C"), "D0": inv_std("D"), "AX": AX,
                        "B3": B3, "B4": B4, "C2": C2}, chain)

        @block.vector
        def _(dve):
            v = nc.vector
            chain = Chain(dve, "dve")
            v.memset(ones[:], 1.0)
            for q in (KA, QA, KC):
                v.memset(q[:].rearrange("p h t -> p (h t)").bitcast(F32), 0.0)
            v.memset(QC[:].rearrange("p h t -> p (h t)").bitcast(F32), 0.0).then_inc(dve_set, 1)
            dve.wait_ge(dve_set, 1)
            v.memset(KA[KS:KM, :, :], 1.0)
            v.memset(KC[KS:KM, :, :], 1.0).then_inc(S["stacks_set"], 1)
            dve.wait_ge(pool_fill, 6)
            v.tensor_copy(identb[:], ident[:]).then_inc(S["idents"], 1)
            dve.wait_ge(S["idents"], 1)

            def ternary(ps, scale, rec, src, dst, n, name, done):
                v.tensor_scalar(scale, ps, 1.0 / n, 1e-5, ALU.mult, ALU.max).then_inc(S[name], 1)
                dve.wait_ge(S[name], 1)
                chain("S", 0, v.reciprocal(rec, scale))
                chain("S", 0, v.tensor_tensor(src, src, rec.unsqueeze(1).broadcast_to(list(src.shape)), ALU.mult))
                chain("S", 0, v.tensor_scalar(src, src, 1.0, -1.0, ALU.min, ALU.max))
                v.tensor_scalar(dst, src, ROUND, ROUND, ALU.add, ALU.subtract).then_inc(S[done], 1)

            def S_(s, t, u):
                dve.wait_ge(S["f1_abs"], 1)
                ps = s.read_big("S")
                ternary(ps[:], f1s[:], wrec[:], f1[:], f1q[:], D, "f1_scale", "f1q")
                dve.wait_ge(S["f2_abs"], 1)
                dve.wait_ge(S["f1q"], 1)
                ps = s.read_small("S")
                ternary(ps[:, 0:D], f2s[:], wrec[:, 0:D], f2[:], f2q[:], HF, "f2_scale", "f2q")

            def stats_of(s, t, stage, x):
                chain(stage, t, v.bn_stats(stats[stage][:], x[:]))
                s.settle()
                chain(stage, t, v.bn_aggr(mv[stage][:], stats[stage][:]))
                v.tensor_scalar(mv[stage][:, 1:2], mv[stage][:, 1:2], EPS, None, ALU.add).then_inc(S[f"var{stage}"], 1)

            def A0(s, t, u):
                wait_in(dve, "x_in", t, u)
                s.before("rstdA", t)
                stats_of(s, t, "A", x0[u])

            def B0(s, t, u):
                s.wait("x1_done", t)
                stats_of(s, t, "B", x1[u])

            def C0(s, t, u):
                s.wait("x2_done", t)
                stats_of(s, t, "C", x2[u])

            def D0(s, t, u):
                s.wait("x3_done", t)
                stats_of(s, t, "D", x3[u])

            def normal(s, t, stage, x):
                s.wait(f"rstd{stage}", t)
                return v.tensor_scalar(xn[stage][:], x[:], mv[stage][:, 0:1], rstd[stage][:], ALU.subtract, ALU.mult)

            def AX(s, t, u):
                s.before("qA", t)
                normal(s, t, "A", x0[u]).then_inc(S["xnA"], 1)

            def BX(s, t, u):
                normal(s, t, "B", x1[u]).then_inc(S["xnB"], 1)

            def CX(s, t, u):
                normal(s, t, "C", x2[u]).then_inc(S["xnC"], 1)

            def quantise(s, t, x, factor, q, dst, name, tmp):
                chain("D", t, v.tensor_reduce(am[:, 0:1], x, FREE, ALU.max, apply_absolute_value=True))
                chain("D", t, v.tensor_scalar(am[:, 1:2], am[:, 0:1], factor, 1e-5, ALU.mult, ALU.max))
                chain("D", t, v.reciprocal(am[:, 2:3], am[:, 1:2]), wait=False)
                chain("D", t, v.tensor_scalar(q[:, 1:2], am[:, 1:2], 1.0 / 127.0, None, ALU.mult))
                chain("D", t, v.tensor_scalar(q[:, 0:1], am[:, 2:3], 127.0 * factor, None, ALU.mult))
                return q

            def DX(s, t, u):
                chain("D", t, normal(s, t, "D", x3[u]))
                quantise(s, t, xn["D"][:], 1.0, qs1, None, None, None)
                chain("D", t, v.tensor_scalar(xn["D"][:], xn["D"][:], qs1[:, 0:1], ROUND, ALU.mult, ALU.add))
                v.tensor_scalar(yq[:], xn["D"][:], ROUND, 127.0, ALU.subtract, ALU.min).then_inc(S["yq"], 1)

            def A1(s, t, u):
                for j in range(5):
                    ps = s.read_small("A1", j)
                    dst = KA[0:K0, :, :] if j == 0 else QA[0:K0, 8 * (j - 1):8 * j, :]
                    v.tensor_copy(dst, ps[:].bitcast(BF16).rearrange("p (h t) -> p h t", t=P)[0:K0]).then_inc(S["KA_QA"], 1)

            def neg_max(s, part, j, dst, name):
                ps = s.read_big(part, j)
                v.tensor_reduce(dst[:, 8 * j:8 * (j + 1)], ps[:].rearrange("p (h t) -> p h t", t=P), FREE, ALU.max,
                                negate=True).then_inc(S[name], 1)

            def two_parts(s, t, stage, x, parts, x_name, per_tile, name):
                s.wait(x_name, t, per_tile)
                chain(stage, t, v.tensor_copy(parts[:, 0, :], x[:]))
                v.tensor_tensor(parts[:, 1, :], x[:], parts[:, 0, :], ALU.subtract).then_inc(S[name], 1)

            def A2(s, t, u):
                for j in range(4):
                    neg_max(s, "A2", j, nmA, "nmA")
                two_parts(s, t, "A", nmA, nm2A, "nmA", 4, "nm2A")

            def C4(s, t, u):
                for j in range(2):
                    neg_max(s, "C4", j, nmC, "nmC")
                two_parts(s, t, "C", nmC, nm2C, "nmC", 2, "nm2C")

            def A6(s, t, u):
                for r in range(2):
                    ps = s.read_small("A6", r)[:].rearrange("p (g j c) -> p g j c", g=G0, c=SLOT)
                    rl = rlA[:, r, :].rearrange("p (g j) -> p g j", g=G0)
                    if r == 0:
                        chain("A", t, v.reciprocal(rl.unsqueeze(3), ps[:, :, :, ONE0:ONE0 + 1]))
                    else:
                        v.reciprocal(rl.unsqueeze(3), ps[:, :, :, ONE0:ONE0 + 1]).then_inc(S["rlA"], 1)
                        s.wait("rlA", t)
                    dst = oA[:, r * P:(r + 1) * P].rearrange("p (j g d) -> p g j d", j=4, g=G0)
                    v.tensor_tensor(dst, ps[:, :, :, 0:HD0], rl.unsqueeze(3).broadcast_to([P, G0, 4, HD0]), ALU.mult)\
                        .then_inc(S["oA"], 1)
                s.wait("oA", t, 2)
                v.tensor_tensor(x1[u][:], oA[:], x0[u][:], ALU.add).then_inc(S["x1_done"], 1)

            def gated(ps, t_, lo, n):
                return v.scalar_tensor_tensor(out=uB[:, lo:lo + n], in0=tB[:, lo:lo + n], scalar=1.0, in1=ps[:, 0:n],
                                              op0=ALU.add, op1=ALU.mult)

            def B2(s, t, u):
                s.wait("gate_exp", t)
                ch = lambda ins: chain("B", t, ins)
                ch(v.tensor_scalar(rt["den"][:], eB[:], 1.0, None, ALU.add))
                ch(v.reciprocal(rt["score"][:], rt["den"][:]))
                v.tensor_scalar(rt["half"][:], rt["score"][:], 0.5, None, ALU.mult).then_inc(S["score"], 1)
                if isinstance(t, int) and t == 0:
                    dve.wait_ge(S["bias_in"], 16)
                    dve.wait_ge(S["consts"], 2)
                ch(v.tensor_tensor(rt["v"][:], rt["score"][:], bias[:], ALU.add))
                other = rt["v"][:].unsqueeze(1).broadcast_to([P, E, E])
                own = rt["v"][:].unsqueeze(2).broadcast_to([P, E, E])
                chain("B", t, v.tensor_tensor(gt[:], other, own, ALU.is_gt), wait=False)
                ch(v.tensor_tensor(eq[:], other, own, ALU.is_equal))
                ch(v.tensor_tensor(eq[:], eq[:], before[:], ALU.mult))
                ch(v.tensor_tensor(gt[:], gt[:], eq[:], ALU.add))
                ch(v.tensor_reduce(rt["rank"][:], gt[:], FREE, ALU.add))
                ch(v.scalar_tensor_tensor(out=rt["sel"][:], in0=rt["rank"][:], scalar=1.5, in1=rt["score"][:],
                                          op0=ALU.is_lt, op1=ALU.mult))
                v.tensor_tensor(rt["c"][:], rt["sel"][:], rt["half"][:], ALU.mult).then_inc(S["route_c"], 1)
                ps = s.read_big("B2")
                s.wait("tB", t, 3, 1)
                ch(gated(ps, t, E * HID, HID))
                v.scalar_tensor_tensor(out=hB[:, E * HID:], in0=uB[:, E * HID:], scalar=0.5, in1=ps[:, BANK:BANK + HID],
                                       op0=ALU.mult, op1=ALU.mult).then_inc(S["vB"], 1)

            def products(s, part, t, e0, k):
                ps = s.read_big(part)
                s.wait("tB", t, 3, k)
                chain("B", t, gated(ps, t, e0 * HID, BANK))
                v.tensor_tensor(vB[:, e0 * HID:e0 * HID + BANK], uB[:, e0 * HID:e0 * HID + BANK], ps[:, BANK:],
                                ALU.mult).then_inc(S["vB"], 1)

            def B3(s, t, u):
                s.before("hB", t, 2)
                products(s, "B3", t, 0, 2)

            def B4(s, t, u):
                products(s, "B4", t, 4, 3)

            def B6(s, t, u):
                ps = s.read_small("B6")
                v.tensor_tensor(x2[u][:], ps[:, 0:D], x1[u][:], ALU.add).then_inc(S["x2_done"], 1)

            def C2(s, t, u):
                def heads(x):
                    return x.rearrange("p (h d) -> p h d", h=H1)

                ps = s.read_small("C2", 0)
                s.wait("qC_hi", t)
                v.tensor_tensor(heads(qrC[:]), heads(ps[:, 0:D]), qC[:, :, 0, :], ALU.subtract).then_inc(S["qC_rest"], 1)
                ps = s.read_small("C2", 1)
                s.wait("VC", t)
                v.tensor_tensor(heads(krC[:]), heads(ps[:, 0:D]), kC[:, :, 1, :], ALU.subtract).then_inc(S["kC_rest"], 1)

            def C8(s, t, u):
                ps = s.read_small("C8")[:].rearrange("p (h c) -> p h c", c=SLOT)
                v.reciprocal(rlC[:].unsqueeze(2), ps[:, :, ONE1:ONE1 + 1]).then_inc(S["rlC"], 1)
                s.wait("rlC", t)
                v.tensor_tensor(oC[:].rearrange("p (h d) -> p h d", d=HD1), ps[:, :, 0:HD1],
                                rlC[:].unsqueeze(2).broadcast_to([P, H1, HD1]), ALU.mult).then_inc(S["oC"], 1)

            def C10(s, t, u):
                ps = s.read_small("C10")
                v.tensor_tensor(x3[u][:], ps[:, 0:D], x2[u][:], ALU.add).then_inc(S["x3_done"], 1)

            def D1(s, t, u):
                ps = s.read_small("D1")
                v.tensor_copy(yT[:].rearrange("p c t -> p (c t)"), ps[:].bitcast(BF16)[:, 0:D]).then_inc(S["yT"], 1)

            def D2(s, t, u):
                ps = s.read_big("D2")
                v.scalar_tensor_tensor(out=z[:], in0=ps[:], scalar=qs1[:, 1:2], in1=f1s[:], op0=ALU.mult, op1=ALU.mult)\
                    .then_inc(S["z"], 1)

            def D2b(s, t, u):
                s.wait("zz", t)
                v.scalar_tensor_tensor(out=inner[:], in0=zz[:], scalar=1.0, in1=z[:], op0=ALU.add, op1=ALU.mult)\
                    .then_inc(S["inner"], 1)

            def D2c(s, t, u):
                s.wait("th", t)
                chain("D", t, v.scalar_tensor_tensor(out=g2[:], in0=th[:], scalar=1.0, in1=z[:], op0=ALU.add, op1=ALU.mult))
                quantise(s, t, g2[:], 0.5, qs2, None, None, None)
                chain("D", t, v.tensor_scalar(g2[:], g2[:], qs2[:, 0:1], ROUND, ALU.mult, ALU.add))
                v.tensor_scalar(gq[:], g2[:], ROUND, 127.0, ALU.subtract, ALU.min).then_inc(S["gq"], 1)

            def D3(s, t, u):
                ps = s.read_small("D3")
                v.tensor_copy(gT[:].rearrange("p k t -> p (k t)"), ps[:].bitcast(BF16)).then_inc(S["gT"], 1)

            def D4(s, t, u):
                if not (isinstance(t, int) and t < 2):
                    dve.wait_ge(S[f"stored{u}"], (t - u) * 8)
                ps = s.read_small("D4")
                v.scalar_tensor_tensor(out=xn["D"][:], in0=ps[:, 0:D], scalar=qs2[:, 1:2], in1=f2s[:], op0=ALU.mult,
                                       op1=ALU.mult).then_inc(S["y2"], 1)
                s.wait("y2", t)
                v.tensor_tensor(x4[u][:], xn["D"][:], x3[u][:], ALU.add).then_inc(S["x4_done"], 1)

            walk(dve, {"S": S_, "A0": A0, "B0": B0, "C0": C0, "D0": D0, "AX": AX, "BX": BX, "CX": CX, "DX": DX, "A1": A1,
                       "A2": A2, "A6": A6, "B2": B2, "B3": B3, "B4": B4, "B6": B6, "C2": C2, "C4": C4, "C8": C8,
                       "C10": C10, "D1": D1, "D2": D2, "D2b": D2b, "D2c": D2c, "D3": D3, "D4": D4}, chain)


def kernel(**inputs):
    import concourse.bacc as bacc
    from concourse.bass_utils import run_bass_kernel_spmd

    get = {k: np.asarray(v) for k, v in inputs.items()}
    x = get["x"]
    tiles = x.shape[0]

    def laid(v, *shape):
        return np.ascontiguousarray(v).reshape(shape)

    arrays = {
        "x": laid(x, tiles, P, D),
        "ctx": laid(get["ctx_512"], tiles, P, L),
        "ctxT": laid(get["ctx_512"].transpose(0, 2, 1), tiles, L, P),
        "bias": laid(get["L0_ffn_expert_bias"], E),
        "gateT": laid(get["L0_ffn_gate_w"].T, DC, P, E),
        "w1T": laid(get["L0_ffn_w1"].transpose(2, 0, 1), DC, P, E * HID),
        "w3T": laid(get["L0_ffn_w3"].transpose(2, 0, 1), DC, P, E * HID),
        "w2T": laid(get["L0_ffn_w2"].transpose(0, 2, 1), E, HID, D),
        "sw1T": laid(get["L0_ffn_sw1"].T, DC, P, HID),
        "sw3T": laid(get["L0_ffn_sw3"].T, DC, P, HID),
        "sw2T": laid(get["L0_ffn_sw2"].T, HID, D),
        "WqT": laid(get["L1_xattn_Wq"].T, DC, P, D),
        "WkvT": laid(get["L1_xattn_Wkv_expand"].T, L, 2 * D),
        "WoutT": laid(get["L1_xattn_Wout"].T, DC, P, D),
        "f1T": laid(get["L1_ffn_w1"].T, DC, P, HF),
        "f2T": laid(get["L1_ffn_w2"].T, FC, P, D),
    }
    nc = bacc.Bacc("TRN2", target_bir_lowering=False, num_devices=1)
    a = {k: nc.dram_tensor(f"in_{k}", v.shape, F32, kind="ExternalInput").ap() for k, v in arrays.items()}
    out = nc.dram_tensor("out", (tiles, P, D), F32, kind="ExternalOutput").ap()
    build(nc, a, out, tiles)
    r = run_bass_kernel_spmd(nc, [{f"in_{k}": v for k, v in arrays.items()}], core_ids=[0])
    return r.results[0]["out"]
```

```python
from contextlib import ExitStack

import numpy as np

import concourse.bass as bass
from concourse import mybir

F32 = mybir.dt.float32
BF16 = mybir.dt.bfloat16
ALU = mybir.AluOpType
ACT = mybir.ActivationFunctionType
FREE = mybir.AxisListType.X

P = 128
D = 256
DC = D // P
L = 64
LK = 96
EPS = 1e-5
BANK = 512

KV0, G0, HD0 = 8, 4, 8
H0 = KV0 * G0
H1, HD1 = 16, 16
SLOT = 32
ONE0, ONE1 = HD0, HD1
NP = 6
K0, K1 = NP * HD0, NP * HD1
HALF = P // 2
Q_PARTS = (slice(0, 3), slice(3, 5), slice(5, 6))
K_PARTS = (slice(1, 6, 2), slice(2, 5, 2), slice(0, 1))
KM = K1 + 2

E, HID = 8, 128
NE = E + 1
GROUPS = ((8, 1), (0, 4), (4, 4))
HF = 1024
FC = HF // P

ROUND = 12582912.0
MASK = -3.0e38

SMALL_RING, BIG_RING = 4, 2

PARTS = {
    "S1": (1, "f1_scale", 1, 1), "S2": (0, "f2_scale", 1, 1),
    "A1.0": (0, "KA_QA", 4, 2), "A1.1": (0, "KA_QA", 4, 3), "A1.2": (0, "KA_QA", 4, 4),
    "A2.0": (1, "nmA", 4, 1), "A2.1": (1, "nmA", 4, 2), "A2.2": (1, "nmA", 4, 3),
    "A2.3": (1, "nmA", 4, 4), "A3": (0, "mTA", 1, 1), "A4.0": (1, "PA", 4, 1), "A4.1": (1, "PA", 4, 2),
    "A4.2": (1, "PA", 4, 3), "A4.3": (1, "PA", 4, 4), "A5.0": (0, "OA", 2, 1), "A5.1": (0, "OA", 2, 2),
    "A6.0": (0, "oA", 2, 1), "A6.1": (0, "oA", 2, 2),
    "B1": (0, "xTB", 1, 1), "B2": (1, "vB", 3, 1), "B3": (1, "vB", 3, 2), "B4": (1, "vB", 3, 3),
    "B5.0": (0, "hTB", 3, 1), "B5.1": (0, "hTB", 3, 2), "B5.2": (0, "hTB", 3, 3), "B6": (0, "x2_done", 1, 1),
    "C1": (0, "xTC", 1, 1), "C2.0": (0, "qC_rest", 1, 1), "C2.1": (0, "kC_rest", 1, 1), "C3.0": (0, "KC_QC", 4, 1),
    "C3.1": (0, "KC_QC", 4, 2), "C3.2": (0, "KC_QC", 4, 3), "C3.3": (0, "KC_QC", 4, 4), "C4.0": (1, "nmC", 2, 1),
    "C4.1": (1, "nmC", 2, 2), "C5": (0, "mTC", 1, 1), "C6.0": (1, "PC", 2, 1), "C6.1": (1, "PC", 2, 2),
    "C7": (0, "OC", 1, 1), "C8": (0, "oC", 1, 1), "C9": (0, "oTC", 1, 1), "C10": (0, "x3_done", 1, 1),
    "D1": (0, "yT", 1, 1), "D2": (1, "z", 1, 1), "D3": (0, "gT", 1, 1), "D4": (0, "y2", 1, 1),
}
PROGRAMS = {
    "sync": """
        D4/6 A6.1/2 A3/1 C0/2 C5/3
        """,
    "tensor": """
        C9/5 B1/3 C2.1/4 C10/5 A2.3/2 B2/3 C3.0/4 S1 C3.1/4 B3/3 A3/2 B4/3 D3/6 C3.2/4 D1/5 C3.3/4 B5.0/3 D2/5 B5.1/3
        C4.0/4 C4.1/4 B5.2/3 A4.0/2 D4/6 A4.1/2 C5/4 B6/3 A4.2/2 A4.3/2 A5.0/2 C6.0/4 A1.0/1 C6.1/4 A5.1/2 A1.1/1
        A6.0/2 A6.1/2 C7/4 A1.2/1 C1/3 A2.0/1 C8/4 C2.0/3 A2.1/1 S2 A2.2/1
        """,
    "scalar": """
        C6.0/5 C6.1/5 S1 A5.0/3 A5.1/3 C7/5 C1/4 C2.0/4 C9/5 B1/3 C2.1/4 B2/3 B3/3 A3/2 C3.0/4 C3.1/4 B4/3 C3.2/4 S2
        C3.3/4 B5.0/3 B5.1/3 D2/5 B5.2/3 A4.0/2 A4.1/2 C5/4 D2b/5 AX/1 A4.2/2 A4.3/2
        """,
    "gpsimd": """
        C6.0/5 C6.1/5 C0/4 B0/3 C2.0/4 D0/5 C2.1/4 B3/3 A0/1 B4/3 AX/1
        """,
    "vector": """
        S1 D4/6 D2c/5 B6/3 A1.0/1 C0/3 A1.1/1 A6.0/2 A6.1/2 CX/3 B0/2 A1.2/1 A2.0/1 C8/4 BX/2 C2.0/3 A2.1/1 A2.2/1
        C10/4 A2.3/1 B2/2 C2.1/3 D0/4 A0 DX/4 B3/2 D3/5 D1/4 B4/2 D2/4 C4.0/3 C4.1/3 D2b/4 AX S2
        """,
}
SETUP_SLOT = 2
CHAIN = {
    "dve": {"S1": 3, "S2": 3, "A0": 2, "A2.3": 1, "A6.0": 1, "A6.1": 1, "B0": 2, "B2": 10, "B3": 1, "B4": 1,
            "C0": 2, "C4.1": 1, "D0": 2, "DX": 7, "D2c": 7},
    "pool": {"AX": 6, "C2.0": 2, "C2.1": 2},
}


def parsed(text):
    for word in text.split():
        part, _, lag = word.partition("/")
        yield part, int(lag or 0) if part[0] != "S" else SETUP_SLOT


PROGRAM = {engine: list(parsed(text)) for engine, text in PROGRAMS.items()}
LAG = {engine: dict(program) for engine, program in PROGRAM.items()}
LAST_LAG = max(max(lag.values()) for lag in LAG.values())


def active(part, n, tiles, lag):
    return n == SETUP_SLOT if part[0] == "S" else 0 <= n - lag < tiles


def ring_uses(tiles, which, size):
    at, order = {}, []
    for n in range(tiles + LAST_LAG):
        for part, lag in PROGRAM["tensor"]:
            if active(part, n, tiles, lag) and PARTS[part][0] == which:
                at[n - lag, part] = (len(order), order[-size] if len(order) >= size else None)
                order.append((n - lag, part))
    return at


def build(nc, a, out, TILES):
    slots = TILES + LAST_LAG
    first, step = LAST_LAG + 2, 2
    laps = (min(TILES, TILES - 2 + LAG["sync"]["A6.1"]) - first) // step
    uses = [ring_uses(TILES, w, size) for w, size in enumerate((SMALL_RING, BIG_RING))]
    lap_uses = [step * sum(v[0] == w for p, v in PARTS.items() if p[0] != "S") for w in range(2)]
    assert lap_uses[0] % SMALL_RING == 0 and lap_uses[1] % BIG_RING == 0

    with ExitStack() as ctx:
        def sb(name, shape, dt=F32):
            return ctx.enter_context(nc.sbuf_tensor(name, shape, dt))

        def sem(name):
            return ctx.enter_context(nc.semaphore(name))

        big = [ctx.enter_context(nc.psum_tensor(f"big{i}", [P, 2 * BANK], F32)) for i in range(BIG_RING)]
        small = [ctx.enter_context(nc.psum_tensor(f"small{i}", [P, BANK], F32)) for i in range(SMALL_RING)]
        rings = (small, big)
        full = [[sem(f"{name}{i}_full") for i in range(len(ring))] for name, ring in zip(("small", "big"), rings)]

        ident = sb("ident", [P, P])
        identb = sb("identb", [P, P], BF16)
        ones = sb("ones", [P, P])
        mask = sb("mask", [P, P], BF16)
        before = sb("before", [P, E, E])
        bias = sb("bias", [P, E])
        w_ab = [sb(f"w{n}T", [P, DC, E * HID]) for n in (1, 3)]
        w_sg = sb("sw1T_gateT", [P, DC, HID + E])
        w_s3 = sb("sw3T", [P, DC, HID])
        w_2 = sb("w2T", [P, NE, D])
        w_q = sb("WqT", [P, DC, D])
        w_kv = sb("WkvT", [LK, 2 * D])
        w_o = sb("WoutT", [P, DC, D])
        f1 = sb("f1T", [P, DC, HF])
        f2 = sb("f2T", [P, FC, D])
        f1q = sb("f1q", [P, DC, HF], BF16)
        f2q = sb("f2q", [P, FC, D], BF16)
        f1s = sb("f1_scale", [P, HF])
        f2s = sb("f2_scale", [P, D])

        def two(name, shape, dt=F32):
            return [sb(f"{name}_{u}", shape, dt) for u in range(2)]

        x0, x1, x2, x3 = (two(f"x{i}", [P, D]) for i in range(4))
        x4 = two("x4", [P, D])
        cA = two("ctx", [P, L])
        cT = two("ctxT", [LK, P])
        stats = {s: sb(f"stats{s}", [P, 6]) for s in "ABCD"}
        mv = {s: sb(f"mean_var{s}", [P, 2]) for s in "ABCD"}
        rstd = {s: sb(f"rstd{s}", [P, 1]) for s in "ABCD"}
        half = sb("minus_half", [P, 1])
        xn = {s: sb(f"xn{s}", [P, D]) for s in "ABCD"}
        qA = sb("qA", [P, H0, HALF // HD0, HD0], BF16)
        qrA = sb("qrA", [P, D])
        kA = sb("kA", [P, KV0, 2, HALF // HD0, HD0], BF16)
        krA = sb("krA", [P, L])
        KA = sb("KA", [P, KV0, 2, P], BF16)
        QA = sb("QA", [P, H0 // 2, P], BF16)
        nmA = sb("neg_maxA", [P, H0])
        nm2A = sb("neg_max2A", [P, 2, 2, H0 // 2], BF16)
        mTA = sb("neg_maxT_A", [2 * H0, P], BF16)
        VA = two("VA", [P, KV0, SLOT])
        PA = sb("PA", [P, H0, P])
        OA = sb("OA", [P, 2, BANK])
        rlA = sb("rlA", [P, 2, H0 // 2])
        oA = sb("oA", [P, D])
        xTB = sb("xTB", [P, DC, P])
        eB = sb("gate_exp", [P, E])
        rt = {n: sb(f"route_{n}", [P, E]) for n in ("den", "score", "v", "rank", "sel", "half", "c")}
        gt = sb("gt", [P, E, E])
        eq = sb("eq", [P, E, E])
        tB = sb("tB", [P, NE * HID])
        uB = sb("uB", [P, NE * HID])
        vB = sb("vB", [P, NE * HID])
        hB = sb("hB", [P, NE * HID])
        hTB = sb("hTB", [P, NE, P])
        xTC = sb("xTC", [P, DC, P])
        qC = sb("qC", [P, H1, NP, HD1], BF16)
        kC = sb("kC", [P, H1, NP, HD1], BF16)
        qrC = sb("qrC", [P, D])
        krC = sb("krC", [P, D])
        KC = sb("KC", [KM, H1, P], BF16)
        QC = sb("QC", [KM, H1, P], BF16)
        nmC = sb("neg_maxC", [P, H1])
        nm2C = sb("neg_max2C", [P, 2, H1], BF16)
        mTC = sb("neg_maxT_C", [2 * H1, P], BF16)
        VC = sb("VC", [P, H1, SLOT])
        PC = sb("PC", [P, H1, P])
        OC = sb("OC", [P, BANK])
        rlC = sb("rlC", [P, H1])
        oC = sb("oC", [P, D])
        oTC = sb("oTC", [P, DC, P])
        am = sb("amax", [P, 4])
        qs1 = sb("qscale1", [P, 2])
        qs2 = two("qscale2", [P, 2])
        yq = sb("yq", [P, D], BF16)
        yT = sb("yT", [P, DC, P], BF16)
        z = sb("z", [P, HF])
        zz = sb("zz", [P, HF])
        inner = sb("inner", [P, HF])
        th = sb("th", [P, HF])
        g2 = sb("g2", [P, HF])
        y2 = sb("y2", [P, D])
        gq = sb("gq", [P, HF], BF16)
        gT = sb("gT", [P, FC, P], BF16)

        f1a = [x[:] for x in (z, zz)]
        f2a = [x[:, k * D:(k + 1) * D] for x in (inner, th) for k in range(FC // 2)]
        wrec = g2

        w_in = {k: sem(f"w_in_{k}") for k in ("B", "C", "D1", "D2")}
        S = {k: sem(k) for k in (
            "consts", "idents", "stacks_set", "bias_in", "f1_abs", "f2_abs", "f1_scale", "f2_scale", "f1q", "f2q",
            "x_in0", "x_in1", "ctx_in0", "ctx_in1", "v_in0", "v_in1", "ctxT_in0", "ctxT_in1", "stored0", "stored1",
            "varA", "varB", "varC", "varD", "rstdA", "rstdB", "rstdC", "rstdD", "xnA", "xnB", "xnC",
            "kA_hi", "qA_hi", "kA", "kA_both", "qA", "KA_QA", "nmA", "nm2A", "mTA", "mrowsA", "PA", "OA", "oA",
            "x1_done",
            "xTB", "gate_exp", "score", "route_c", "tB", "vB", "hB", "hTB", "x2_done",
            "xTC", "qC_hi", "kC_hi", "VC", "qC_rest", "kC_rest", "qC", "kC", "KC_QC", "nmC", "nm2C", "mTC", "mrowsC",
            "PC", "PC_causal", "OC", "rlC", "oC", "oTC", "x3_done",
            "yq", "yT", "z", "zz", "inner", "th", "gq", "gT", "y2", "x4_done")}
        chain_sem = {(e, s): sem(f"{e}_step_{s}") for e in CHAIN for s in CHAIN[e]}

        pool_fill, dve_set, settled = sem("pool_fill"), sem("dve_set"), sem("settled")

        class Slot:

            def __init__(self, eng, n, lap=None):
                self.eng, self.n, self.lap = eng, n, lap

            def start(self, part, lag):
                self.part, self.first_tile = part, self.n - lag
                return self.at(self.first_tile, step), self.first_tile % 2

            def at(self, base, per_lap):
                return base if self.lap is None else base + self.lap * per_lap

            def wait(self, name, t, per_tile=1, k=None):
                self.eng.wait_ge(S[name], t * per_tile + (per_tile if k is None else k))

            def settle(self):
                self.eng.sem_inc(settled, 1)

            def before(self, name, t, per_tile=1):
                if not (isinstance(t, int) and t == 0):
                    self.eng.wait_ge(S[name], t * per_tile)

            def fill(self, part):
                which = PARTS[part][0]
                use, prior = uses[which][self.first_tile, part]
                if prior is not None:
                    tile, p = prior
                    _, name, per_tile, k = PARTS[p]
                    self.eng.wait_ge(S[name], self.at(tile * per_tile + k, step * per_tile))
                b = use % len(rings[which])
                return rings[which][b], full[which][b]

            def read(self, part):
                which = PARTS[part][0]
                use, size = uses[which][self.first_tile, part][0], len(rings[which])
                self.eng.wait_ge(full[which][use % size], self.at(use // size + 1, lap_uses[which] // size))
                return rings[which][use % size]

        class Chain:

            def __init__(self, eng, kind):
                self.eng, self.per, self.kind = eng, CHAIN[kind], kind
                self.done = dict.fromkeys(self.per, 0)

            def __call__(self, slot, t, ins, wait=True):
                part = slot.part
                ins.then_inc(chain_sem[self.kind, part], 1)
                self.done[part] += 1
                if wait:
                    self.eng.wait_ge(chain_sem[self.kind, part], t * self.per[part] + self.done[part])

            def end_slot(self):
                for s, k in self.done.items():
                    assert k in (0, self.per[s]), (self.kind, s, k)
                    self.done[s] = 0

        def walk(eng, engine, parts, chain=None):
            def emit(n, lap=None):
                slot = Slot(eng, n, lap)
                for part, lag in PROGRAM[engine]:
                    if active(part, n, TILES, lag):
                        name, _, j = part.partition(".")
                        tile, buffer = slot.start(part, lag)
                        parts[name](slot, tile, buffer, *([int(j)] if j else []))
                if chain:
                    chain.end_slot()

            n = 0
            while n < slots:
                if laps and n == first:
                    with eng.Fori(0, laps) as lap:
                        for i in range(step):
                            emit(first + i, lap)
                    n += laps * step
                else:
                    emit(n)
                    n += 1

        def wait_in(eng, name, t, u):
            eng.wait_ge(S[f"{name}{u}"], (t + (2 - u)) * 8)

        block = ctx.enter_context(nc.Block())

        @block.sync
        def _(sp):
            def load(u, t):
                sp.dma_start(x0[u][:], a["x"][t]).then_inc(S[f"x_in{u}"], 16)
                sp.dma_start(cA[u][:], a["ctx"][t]).then_inc(S[f"ctx_in{u}"], 16)
                sp.dma_start(VA[u][:, :, 0:HD0], a["ctx"][t].rearrange("p (h d) -> p h d", d=HD0))\
                    .then_inc(S[f"v_in{u}"], 16)

            def S_load():
                sp.dma_start(bias[:], a["bias"].unsqueeze(0).broadcast_to([P, E])).then_inc(S["bias_in"], 16)
                for c in range(DC):
                    sp.dma_start(w_sg[:, c, 0:HID], a["sw1T"][c]).then_inc(w_in["B"], 16)
                    sp.dma_start(w_sg[:, c, HID:HID + E], a["gateT"][c]).then_inc(w_in["B"], 16)
                    sp.dma_start(w_s3[:, c, :], a["sw3T"][c]).then_inc(w_in["B"], 16)
                    sp.dma_start(w_ab[0][:, c, :], a["w1T"][c]).then_inc(w_in["B"], 16)
                    sp.dma_start(w_ab[1][:, c, :], a["w3T"][c]).then_inc(w_in["B"], 16)
                sp.dma_start(w_2[:, 0:E, :], a["w2T"].rearrange("e h d -> h e d")).then_inc(w_in["B"], 16)
                sp.dma_start(w_2[:, E, :], a["sw2T"]).then_inc(w_in["B"], 16)
                for c in range(DC):
                    sp.dma_start(f1[:, c, :], a["f1T"][c]).then_inc(w_in["D1"], 16)
                sp.dma_start(f2[:], a["f2T"].rearrange("k p d -> p k d")).then_inc(w_in["D2"], 16)
                for c in range(DC):
                    sp.dma_start(w_q[:, c, :], a["WqT"][c]).then_inc(w_in["C"], 16)
                    sp.dma_start(w_o[:, c, :], a["WoutT"][c]).then_inc(w_in["C"], 16)
                sp.dma_start(w_kv[0:L, :], a["WkvT"]).then_inc(w_in["C"], 16)

            sp.wait_ge(S["consts"], 1)
            load(0, 0)
            S_load()
            load(1, 1)

            def A3(s, t, u):
                s.wait("mTA", t)
                for i in range(2):
                    sp.dma_start(QA[i * HALF + K0:i * HALF + K0 + 2, :, :], mTA[i * H0:(i + 1) * H0, :])\
                        .then_inc(S["mrowsA"], 16)

            def C5(s, t, u):
                s.wait("mTC", t)
                for i in range(2):
                    sp.dma_start(QC[K1 + i:K1 + i + 1, :, :], mTC[i * H1:(i + 1) * H1, :]).then_inc(S["mrowsC"], 16)

            def C0(s, t, u):
                s.before("VC", t)
                sp.dma_start(cT[u][0:L, :], a["ctxT"][t]).then_inc(S[f"ctxT_in{u}"], 16)

            def A6(s, t, u, r):
                if r == 0 or isinstance(t, int) and t + 2 >= TILES:
                    return
                s.wait("x1_done", t)
                load(u, t + 2)

            def D4(s, t, u):
                s.wait("x4_done", t)
                sp.dma_start(out[t], x4[u][:]).then_inc(S[f"stored{u}"], 16)

            walk(sp, "sync", {
                "A3": A3, "C0": C0, "C5": C5, "A6": A6, "D4": D4,
            })
            for u in range(2):
                sp.wait_ge(S[f"stored{u}"], 16 * (TILES // 2))

        @block.tensor
        def _(pe):
            mm, transpose = nc.tensor.matmul, nc.tensor.transpose

            def bf(ps):
                return ps[:].bitcast(BF16)

            def heads_of(ps):
                return bf(ps).rearrange("p (h t) -> p h t", t=P)

            def S1(s, t, u):
                s.eng.wait_ge(S["f1_abs"], DC)
                ps, full = s.fill(s.part)
                for b in range(2):
                    for c in range(DC):
                        last = mm(ps[:, b * BANK:(b + 1) * BANK], ones[:], f1a[c][:, b * BANK:(b + 1) * BANK],
                                  start=(c == 0), stop=(c == DC - 1))
                last.then_inc(full, 1)

            def S2(s, t, u):
                s.eng.wait_ge(S["f2_abs"], 2)
                ps, full = s.fill(s.part)
                for k in range(FC):
                    last = mm(ps[:, 0:D], ones[:], f2a[k], start=(k == 0), stop=(k == FC - 1))
                last.then_inc(full, 1)

            def stack(s, columns, rows):
                ps, full = s.fill(s.part)
                s.settle()
                for i in range(8):
                    last = transpose(heads_of(ps)[0:rows, i, :], columns(i), identb[:])
                last.then_inc(full, 1)

            def A1(s, t, u, j):
                if j == 0:
                    s.wait("kA_both", t)
                    stack(s, lambda i: kA[:, i, :, :, :].rearrange("p e i d -> p (e i d)"), P)
                else:
                    s.wait("qA", t)
                    p0 = 2 * 8 * (j - 1)
                    stack(s, lambda i: qA[:, p0 + 2 * i:p0 + 2 * i + 2, :, :].rearrange("p e i d -> p (e i d)"), P)

            def A2(s, t, u, j):
                s.wait("KA_QA", t, 4, 3 + j // 2)
                ps, full = s.fill(s.part)
                for i in range(4):
                    pair = 4 * j + i
                    last = mm(ps[:, 2 * i * P:2 * (i + 1) * P], QA[:, pair, :], KA[:, 2 * pair // G0, :, :],
                              start=True, stop=True)
                last.then_inc(full, 1)

            def A3(s, t, u):
                s.wait("nm2A", t)
                ps, full = s.fill(s.part)
                s.settle()
                transpose(bf(ps)[0:2 * H0, 0:P], nm2A[:].rearrange("p e i h -> p (e i h)"), identb[:]).then_inc(full, 1)

            def A4(s, t, u, j):
                s.wait("mrowsA", t, 32)
                ps, full = s.fill(s.part)
                heads = ps[:].rearrange("p (k h e t) -> p k h e t", k=2, h=2, e=2)
                for i in range(2):
                    kv = 2 * j + i
                    for e in range(2):
                        last = mm(heads[:, i, :, e, :], KA[:, kv, e, :], QA[:, 2 * kv:2 * kv + 2, :], start=True, stop=True)
                last.then_inc(full, 1)

            def A5(s, t, u, r):
                wait_in(pe, "v_in", t, u)
                s.wait("PA", t, 4, 2 * r + 2)
                ps, full = s.fill(s.part)
                for j in range(4):
                    kv = 4 * r + j
                    last = mm(ps[SLOT * j:SLOT * (j + 1), :], VA[u][:, kv, :], PA[:, kv * G0:(kv + 1) * G0, :],
                              start=True, stop=True)
                last.then_inc(full, 1)

            def A6(s, t, u, r):
                s.wait("OA", t, 2, r + 1)
                ps, full = s.fill(s.part)
                for g in range(G0):
                    last = transpose(ps[:, g * P:(g + 1) * P], OA[:, r, g * P:(g + 1) * P], ident[:])
                last.then_inc(full, 1)

            def turn(s, src, idn):
                ps, full = s.fill(s.part)
                dst = ps if src.dtype == F32 else bf(ps)
                for c in range(DC):
                    last = transpose(dst[:, c * P:(c + 1) * P], src[:, c * P:(c + 1) * P], idn[:])
                last.then_inc(full, 1)

            def B1(s, t, u):
                s.wait("xnB", t)
                turn(s, xn["B"], ident)

            def experts(s, wa, wb, na, nb):
                ps, full = s.fill(s.part)
                for w, n, o in ((wa, na, 0), (wb, nb, BANK)):
                    for c in range(DC):
                        last = mm(ps[:, o:o + n], xTB[:, c, :], w[c], start=(c == 0), stop=(c == DC - 1))
                last.then_inc(full, 1)

            def B2(s, t, u):
                if isinstance(t, int) and t == 0:
                    pe.wait_ge(w_in["B"], 16 * (5 * DC + 2))
                s.wait("xTB", t)
                experts(s, [w_sg[:, c, :] for c in range(DC)], [w_s3[:, c, :] for c in range(DC)], HID + E, HID)

            def B3(s, t, u):
                experts(s, *([w[:, c, 0:BANK] for c in range(DC)] for w in w_ab), BANK, BANK)

            def B4(s, t, u):
                experts(s, *([w[:, c, BANK:] for c in range(DC)] for w in w_ab), BANK, BANK)

            def B5(s, t, u, j):
                if j == 0:
                    s.wait("vB", t, 3, 1)
                else:
                    s.wait("hB", t, 2, j)
                ps, full = s.fill(s.part)
                e0, n = GROUPS[j]
                for i in range(n):
                    last = transpose(ps[:, i * P:(i + 1) * P], hB[:, (e0 + i) * HID:(e0 + i + 1) * HID], ident[:])
                last.then_inc(full, 1)

            def B6(s, t, u):
                s.wait("hTB", t, 3)
                ps, full = s.fill(s.part)
                for e in range(NE):
                    last = mm(ps[:, 0:D], hTB[:, e, :], w_2[:, e, :], start=(e == 0), stop=(e == NE - 1))
                last.then_inc(full, 1)

            def C1(s, t, u):
                s.wait("xnC", t)
                turn(s, xn["C"], ident)

            def C2(s, t, u, j):
                ps, full = s.fill(s.part)
                if j == 0:
                    if isinstance(t, int) and t == 0:
                        pe.wait_ge(w_in["C"], 16 * (2 * DC + 1))
                    s.wait("xTC", t)
                    for c in range(DC):
                        last = mm(ps[:, 0:D], xTC[:, c, :], w_q[:, c, :], start=(c == 0), stop=(c == DC - 1))
                else:
                    wait_in(pe, "ctxT_in", t, u)
                    last = mm(ps[:], cT[u][:], w_kv[:], start=True, stop=True)
                last.then_inc(full, 1)

            def C3(s, t, u, j):
                s.wait(("qC", "kC")[j // 2], t)
                src, h0 = (qC, kC)[j // 2], 8 * (j % 2)
                stack(s, lambda i: src[:, h0 + i, :, :].rearrange("p i d -> p (i d)"), K1)

            def C4(s, t, u, j):
                s.wait("KC_QC", t, 4)
                ps, full = s.fill(s.part)
                for b in range(2):
                    mm(ps[:, b * BANK:(b + 1) * BANK], identb[:], mask[:].unsqueeze(1).broadcast_to([P, 4, P]),
                       start=True, stop=False)
                    for i in range(4):
                        h = 8 * j + 4 * b + i
                        last = mm(ps[:, b * BANK + i * P:b * BANK + (i + 1) * P], QC[0:K1, h, :], KC[0:K1, h, :],
                                  start=False, stop=(i == 3))
                last.then_inc(full, 1)

            def C5(s, t, u):
                s.wait("nm2C", t)
                ps, full = s.fill(s.part)
                transpose(bf(ps)[0:2 * H1, 0:P], nm2C[:].rearrange("p i h -> p (i h)"), identb[:]).then_inc(full, 1)

            def C6(s, t, u, j):
                s.wait("mrowsC", t, 32)
                ps, full = s.fill(s.part)
                for i in range(8):
                    h = 8 * j + i
                    last = mm(ps[:, i * P:(i + 1) * P], KC[:, h, :], QC[:, h, :], start=True, stop=True)
                last.then_inc(full, 1)

            def C7(s, t, u):
                s.wait("PC_causal", t, 2)
                ps, full = s.fill(s.part)
                for i in range(4):
                    for j in range(4):
                        h = 4 * i + j
                        last = mm(ps[SLOT * j:SLOT * (j + 1), i * P:(i + 1) * P], VC[:, h, :], PC[:, h, :],
                                  start=True, stop=True)
                last.then_inc(full, 1)

            def C8(s, t, u):
                s.wait("OC", t)
                ps, full = s.fill(s.part)
                for i in range(4):
                    last = transpose(ps[:, i * P:(i + 1) * P], OC[:, i * P:(i + 1) * P], ident[:])
                last.then_inc(full, 1)

            def C9(s, t, u):
                s.wait("oC", t)
                turn(s, oC, ident)

            def C10(s, t, u):
                s.wait("oTC", t)
                ps, full = s.fill(s.part)
                for c in range(DC):
                    last = mm(ps[:, 0:D], oTC[:, c, :], w_o[:, c, :], start=(c == 0), stop=(c == DC - 1))
                last.then_inc(full, 1)

            def D1(s, t, u):
                s.wait("yq", t)
                turn(s, yq, identb)

            def D2(s, t, u):
                if isinstance(t, int) and t == 0:
                    pe.wait_ge(S["f1q"], 1)
                s.wait("yT", t)
                ps, full = s.fill(s.part)
                for b in range(2):
                    for c in range(DC):
                        last = mm(ps[:, b * BANK:(b + 1) * BANK], yT[:, c, :], f1q[:, c, b * BANK:(b + 1) * BANK],
                                  start=(c == 0), stop=(c == DC - 1))
                last.then_inc(full, 1)

            def D3(s, t, u):
                s.wait("gq", t)
                ps, full = s.fill(s.part)
                for k in range(FC):
                    last = transpose(bf(ps)[:, k * P:(k + 1) * P], gq[:, k * P:(k + 1) * P], identb[:])
                last.then_inc(full, 1)

            def D4(s, t, u):
                if isinstance(t, int) and t == 0:
                    pe.wait_ge(S["f2q"], 1)
                s.wait("gT", t)
                ps, full = s.fill(s.part)
                for k in range(FC):
                    last = mm(ps[:, 0:D], gT[:, k, :], f2q[:, k, :], start=(k == 0), stop=(k == FC - 1))
                last.then_inc(full, 1)

            pe.wait_ge(S["idents"], 1)
            pe.wait_ge(S["consts"], 2)
            walk(pe, "tensor", {
                "S1": S1, "S2": S2, "A1": A1, "A2": A2, "A3": A3, "A4": A4, "A5": A5, "A6": A6, "B1": B1,
                "B2": B2, "B3": B3, "B4": B4, "B5": B5, "B6": B6, "C1": C1, "C2": C2, "C3": C3, "C4": C4,
                "C5": C5, "C6": C6, "C7": C7, "C8": C8, "C9": C9, "C10": C10, "D1": D1, "D2": D2, "D3": D3,
                "D4": D4,
            })

        @block.scalar
        def _(act):
            op = nc.scalar.activation

            def S1(s, t, u):
                act.wait_ge(w_in["D1"], 16 * DC)
                for c in range(DC):
                    op(f1a[c], f1[:, c, :], ACT.Abs).then_inc(S["f1_abs"], 1)

            def S2(s, t, u):
                act.wait_ge(w_in["D2"], 16)
                for x, k in ((inner, 0), (th, FC // 2)):
                    op(x[:].rearrange("p (k d) -> p k d", d=D), f2[:, k:k + FC // 2, :], ACT.Abs).then_inc(S["f2_abs"], 1)

            def A3(s, t, u):
                ps = s.read(s.part)
                s.before("mrowsA", t, 32)
                op(mTA[:], ps[:].bitcast(BF16)[0:2 * H0, 0:P], ACT.Copy).then_inc(S["mTA"], 1)

            def C5(s, t, u):
                ps = s.read(s.part)
                s.before("mrowsC", t, 32)
                op(mTC[:], ps[:].bitcast(BF16)[0:2 * H1, 0:P], ACT.Copy).then_inc(S["mTC"], 1)

            def exps(s, j, dst, scale, name):
                ps = s.read(s.part)
                op(dst[:, 8 * j:8 * (j + 1), :], ps[:].rearrange("p (h t) -> p h t", t=P), ACT.Exp,
                   scale=scale).then_inc(S[name], 1)

            def A4(s, t, u, j):
                exps(s, j, PA, float(HD0) ** -0.5, "PA")

            def A5(s, t, u, r):
                ps = s.read(s.part)
                s.before("oA", t, 2)
                op(OA[:, r, :], ps[:], ACT.Copy).then_inc(S["OA"], 1)

            def B1(s, t, u):
                ps = s.read(s.part)
                op(xTB[:].rearrange("p c t -> p (c t)"), ps[:, 0:D], ACT.Copy).then_inc(S["xTB"], 1)

            def B2(s, t, u):
                ps = s.read(s.part)
                op(eB[:], ps[:, HID:HID + E], ACT.Exp, scale=-1.0).then_inc(S["gate_exp"], 1)
                s.before("vB", t, 3)
                op(tB[:, E * HID:], ps[:, 0:HID], ACT.Tanh, scale=0.5).then_inc(S["tB"], 1)

            def silu_tanh(s, t, e0):
                ps = s.read(s.part)
                s.wait("score", t)
                for i in range(4):
                    ins = op(tB[:, (e0 + i) * HID:(e0 + i + 1) * HID], ps[:, i * HID:(i + 1) * HID], ACT.Tanh,
                             scale=rt["half"][:, e0 + i:e0 + i + 1])
                ins.then_inc(S["tB"], 1)

            def B3(s, t, u):
                silu_tanh(s, t, 0)

            def B4(s, t, u):
                silu_tanh(s, t, 4)

            def B5(s, t, u, j):
                ps = s.read(s.part)
                s.before("x2_done", t)
                e0, n = GROUPS[j]
                op(hTB[:, e0:e0 + n, :], ps[:, 0:n * P].rearrange("p (e t) -> p e t", t=P), ACT.Copy)\
                    .then_inc(S["hTB"], 1)

            def C1(s, t, u):
                ps = s.read(s.part)
                op(xTC[:].rearrange("p c t -> p (c t)"), ps[:, 0:D], ACT.Copy).then_inc(S["xTC"], 1)

            def high(dst, where, src, heads):
                n = len(range(NP)[where])
                src = src.rearrange("p (h d) -> p h d", h=heads).unsqueeze(2)
                shape = [P, heads, n, src.shape[3]]
                return op(dst[:, :, where, :], src.broadcast_to(shape), ACT.Copy)

            def AX(s, t, u):
                s.before("KA_QA", t, 4)
                wait_in(act, "ctx_in", t, u)
                high(kA[:, :, 0, :, :], K_PARTS[0], cA[u][:], KV0).then_inc(S["kA_hi"], 1)
                s.wait("xnA", t)
                high(qA, Q_PARTS[0], xn["A"][:], H0).then_inc(S["qA_hi"], 1)
                s.wait("kA", t)
                op(kA[:, :, 1, 0:NP, :], kA[:, :, 0, 0:NP, :], ACT.Copy).then_inc(S["kA_both"], 1)

            def C2(s, t, u, j):
                ps = s.read(s.part)
                s.before("KC_QC", t, 4)
                if j == 0:
                    high(qC, Q_PARTS[0], ps[:, 0:D], H1).then_inc(S["qC_hi"], 1)
                else:
                    high(kC, K_PARTS[0], ps[:, 0:D], H1).then_inc(S["kC_hi"], 1)
                    op(VC[:, :, 0:HD1], ps[:, D:2 * D].rearrange("p (h d) -> p h d", d=HD1), ACT.Copy)\
                        .then_inc(S["VC"], 1)

            def C3(s, t, u, j):
                ps = s.read(s.part)
                op((QC, KC)[j // 2][0:K1, 8 * (j % 2):8 * (j % 2) + 8, :],
                   ps[:].bitcast(BF16).rearrange("p (h t) -> p h t", t=P)[0:K1], ACT.Copy).then_inc(S["KC_QC"], 1)

            def C6(s, t, u, j):
                exps(s, j, PC, float(HD1) ** -0.5, "PC")

            def C7(s, t, u):
                ps = s.read(s.part)
                s.before("oC", t)
                op(OC[:], ps[:], ACT.Copy).then_inc(S["OC"], 1)

            def C9(s, t, u):
                ps = s.read(s.part)
                s.before("x3_done", t)
                op(oTC[:].rearrange("p c t -> p (c t)"), ps[:, 0:D], ACT.Copy).then_inc(S["oTC"], 1)

            def D2(s, t, u):
                s.wait("z", t)
                op(zz[:], z[:], ACT.Square, scale=0.044715 ** 0.5).then_inc(S["zz"], 1)

            def D2b(s, t, u):
                s.wait("inner", t)
                s.before("gq", t)
                op(th[:], inner[:], ACT.Tanh, scale=(2.0 / np.pi) ** 0.5).then_inc(S["th"], 1)

            act.wait_ge(S["stacks_set"], 1)
            walk(act, "scalar", {
                "S1": S1, "S2": S2, "AX": AX, "A3": A3, "A4": A4, "A5": A5, "B1": B1, "B2": B2, "B3": B3,
                "B4": B4, "B5": B5, "C1": C1, "C2": C2, "C3": C3, "C5": C5, "C6": C6, "C7": C7, "C9": C9,
                "D2": D2, "D2b": D2b,
            })

        @block.gpsimd
        def _(pool):
            g = nc.gpsimd
            fills = [0]

            def filled(ins):
                fills[0] += 1
                ins.then_inc(pool_fill, 1)

            def after_fills():
                pool.wait_ge(pool_fill, fills[0])

            for v in VA:
                filled(g.memset(v[:, :, HD0:SLOT], 0.0))
            filled(g.memset(half[:], -0.5))
            filled(g.memset(ident[:], 0.0))
            after_fills()
            filled(g.affine_select(out=ident[:], in_=ident[:], compare_op=ALU.not_equal, fill=1.0, base=0,
                                   pattern=[[-1, P]], channel_multiplier=1))
            for v in VA:
                filled(g.memset(v[:, :, ONE0:ONE0 + 1], 1.0))
            after_fills()
            g.memset(VC[:], 0.0).then_inc(S["consts"], 1)
            filled(g.memset(mask[:], 0.0))
            filled(g.memset(before[:], 0.0))
            pool.wait_ge(S["consts"], 1)
            after_fills()
            filled(g.memset(VC[:, :, ONE1:ONE1 + 1], 1.0))
            filled(g.affine_select(out=mask[:], in_=mask[:], compare_op=ALU.is_ge, fill=MASK, base=0,
                                   pattern=[[-1, P]], channel_multiplier=1))
            g.affine_select(out=before[:], in_=before[:], compare_op=ALU.is_ge, fill=1.0, base=0,
                            pattern=[[-1, E], [1, E]], channel_multiplier=0).then_inc(S["consts"], 1)
            after_fills()

            chain = Chain(pool, "pool")

            def inv_std(stage):
                def part(s, t, u):
                    s.wait(f"var{stage}", t)
                    g.tensor_tensor(rstd[stage][:], mv[stage][:, 1:2], half[:], ALU.pow).then_inc(S[f"rstd{stage}"], 1)
                return part

            def lower(s, t, dst, where, rest, heads, name):
                rest = rest[:].rearrange("p (h d) -> p h d", h=heads)
                mid, low = dst[:, :, where[1], :], dst[:, :, where[2], :]
                s.settle()
                for i in range(2):
                    chain(s, t, g.tensor_copy(mid[:, :, i, :], rest), wait=(i == 1))
                g.tensor_tensor(low[:, :, 0, :], rest, mid[:, :, 0, :], ALU.subtract).then_inc(S[name], 1)

            def AX(s, t, u):
                s.before("KA_QA", t, 4)
                for x, name, dst, where, rest, heads in ((cA[u], "kA", kA[:, :, 0, :, :], K_PARTS, krA, KV0),
                                                         (xn["A"], "qA", qA, Q_PARTS, qrA, H0)):
                    s.wait(f"{name}_hi", t)
                    high = dst[:, :, where[0], :][:, :, 0, :]
                    chain(s, t, g.tensor_tensor(rest[:].rearrange("p (h d) -> p h d", h=heads),
                                                  x[:].rearrange("p (h d) -> p h d", h=heads), high, ALU.subtract))
                    lower(s, t, dst, where, rest, heads, name)

            def B3(s, t, u):
                s.wait("route_c", t)
                s.before("hTB", t, 3)
                weigh(s, t, 0, 2, 1)

            def B4(s, t, u):
                weigh(s, t, 4, 3, 2)

            def weigh(s, t, e0, k, done):
                s.wait("vB", t, 3, k)
                sl = slice(e0 * HID, (e0 + 4) * HID)
                g.tensor_tensor(hB[:, sl].rearrange("p (e h) -> p e h", e=4), vB[:, sl].rearrange("p (e h) -> p e h", e=4),
                                rt["c"][:, e0:e0 + 4].unsqueeze(2).broadcast_to([P, 4, HID]), ALU.mult)\
                    .then_inc(S["hB"], 1)

            def C2(s, t, u, j):
                if j == 0:
                    s.wait("qC_rest", t)
                    lower(s, t, qC, Q_PARTS, qrC, H1, "qC")
                else:
                    s.wait("kC_rest", t)
                    lower(s, t, kC, K_PARTS, krC, H1, "kC")

            def C6(s, t, u, j):
                s.wait("PC", t, 2, j + 1)
                s.settle()
                p = PC[:, 8 * j:8 * (j + 1), :]
                g.affine_select(out=p, in_=p, compare_op=ALU.is_ge, fill=0.0, base=0, pattern=[[0, 8], [1, P]],
                                channel_multiplier=-1).then_inc(S["PC_causal"], 1)

            walk(pool, "gpsimd", {
                "C6": C6, "A0": inv_std("A"), "B0": inv_std("B"), "C0": inv_std("C"), "D0": inv_std("D"),
                "AX": AX, "B3": B3, "B4": B4, "C2": C2,
            }, chain)

        @block.vector
        def _(dve):
            v = nc.vector
            chain = Chain(dve, "dve")
            v.memset(ones[:], 1.0)
            v.memset(KA[:], 0.0)
            for x in (w_kv, *cT):
                v.memset(x[L:LK, :], 0.0)
            v.memset(qA[:, :, NP:, :], 0.0)
            v.memset(kA[:, :, :, NP:, :], 0.0).then_inc(dve_set, 1)
            dve.wait_ge(dve_set, 1)
            v.memset(kA[:, :, :, NP, 0:2], 1.0)
            v.memset(KC[K1:KM, :, :], 1.0).then_inc(S["stacks_set"], 1)
            dve.wait_ge(pool_fill, 6)
            v.tensor_copy(identb[:], ident[:]).then_inc(S["idents"], 1)
            dve.wait_ge(S["idents"], 1)

            def ternary(s, ps, scale, rec, src, dst, n, name, done):
                v.tensor_scalar(scale, ps, 1.0 / n, 1e-5, ALU.mult, ALU.max).then_inc(S[name], 1)
                dve.wait_ge(S[name], 1)
                chain(s, 0, v.reciprocal(rec, scale))
                chain(s, 0, v.tensor_tensor(src, src, rec.unsqueeze(1).broadcast_to(list(src.shape)), ALU.mult))
                chain(s, 0, v.tensor_scalar(src, src, 1.0, -1.0, ALU.min, ALU.max))
                v.tensor_scalar(dst, src, ROUND, ROUND, ALU.add, ALU.subtract).then_inc(S[done], 1)

            def S1(s, t, u):
                dve.wait_ge(S["f1_abs"], DC)
                ps = s.read(s.part)
                ternary(s, ps[:], f1s[:], wrec[:], f1[:], f1q[:], D, "f1_scale", "f1q")

            def S2(s, t, u):
                dve.wait_ge(S["f2_abs"], 2)
                dve.wait_ge(S["f1q"], 1)
                ps = s.read(s.part)
                ternary(s, ps[:, 0:D], f2s[:], wrec[:, 0:D], f2[:], f2q[:], HF, "f2_scale", "f2q")

            def stats_of(s, t, stage, x):
                chain(s, t, v.bn_stats(stats[stage][:], x[:]))
                s.settle()
                chain(s, t, v.bn_aggr(mv[stage][:], stats[stage][:]))
                v.tensor_scalar(mv[stage][:, 1:2], mv[stage][:, 1:2], EPS, None, ALU.add).then_inc(S[f"var{stage}"], 1)

            def A0(s, t, u):
                wait_in(dve, "x_in", t, u)
                s.before("rstdA", t)
                stats_of(s, t, "A", x0[u])

            def B0(s, t, u):
                s.wait("x1_done", t)
                stats_of(s, t, "B", x1[u])

            def C0(s, t, u):
                s.wait("x2_done", t)
                stats_of(s, t, "C", x2[u])

            def D0(s, t, u):
                s.wait("x3_done", t)
                stats_of(s, t, "D", x3[u])

            def normal(s, t, stage, x):
                s.wait(f"rstd{stage}", t)
                return v.tensor_scalar(xn[stage][:], x[:], mv[stage][:, 0:1], rstd[stage][:], ALU.subtract, ALU.mult)

            def AX(s, t, u):
                s.before("qA", t)
                normal(s, t, "A", x0[u]).then_inc(S["xnA"], 1)

            def BX(s, t, u):
                normal(s, t, "B", x1[u]).then_inc(S["xnB"], 1)

            def CX(s, t, u):
                normal(s, t, "C", x2[u]).then_inc(S["xnC"], 1)

            def quantise(s, t, x, factor, q):
                chain(s, t, v.tensor_reduce(am[:, 0:1], x, FREE, ALU.max, apply_absolute_value=True))
                chain(s, t, v.tensor_scalar(am[:, 1:2], am[:, 0:1], factor, 1e-5, ALU.mult, ALU.max))
                chain(s, t, v.reciprocal(am[:, 2:3], am[:, 1:2]), wait=False)
                chain(s, t, v.tensor_scalar(q[:, 1:2], am[:, 1:2], 1.0 / 127.0, None, ALU.mult))
                chain(s, t, v.tensor_scalar(q[:, 0:1], am[:, 2:3], 127.0 * factor, None, ALU.mult))

            def DX(s, t, u):
                chain(s, t, normal(s, t, "D", x3[u]))
                quantise(s, t, xn["D"][:], 1.0, qs1)
                chain(s, t, v.tensor_scalar(xn["D"][:], xn["D"][:], qs1[:, 0:1], ROUND, ALU.mult, ALU.add))
                v.tensor_scalar(yq[:], xn["D"][:], ROUND, 127.0, ALU.subtract, ALU.min).then_inc(S["yq"], 1)

            def A1(s, t, u, j):
                ps = s.read(s.part)
                s.before("PA", t, 4)
                heads = ps[:].bitcast(BF16).rearrange("p (h t) -> p h t", t=P)
                if j == 0:
                    for e in range(2):
                        half = slice(e * HALF, (e + 1) * HALF)
                        v.tensor_copy(KA[half, :, e, :], heads[half]).then_inc(S["KA_QA"], 1)
                else:
                    v.tensor_copy(QA[:, 8 * (j - 1):8 * j, :], heads).then_inc(S["KA_QA"], 1)

            def neg_max(s, j, dst, name):
                ps = s.read(s.part)
                v.tensor_reduce(dst[:, 8 * j:8 * (j + 1)], ps[:].rearrange("p (h t) -> p h t", t=P), FREE, ALU.max,
                                negate=True).then_inc(S[name], 1)

            def two_parts(s, t, x, parts, x_name, per_tile, name):
                s.wait(x_name, t, per_tile)
                chain(s, t, v.tensor_copy(parts[0], x))
                v.tensor_tensor(parts[1], x, parts[0], ALU.subtract).then_inc(S[name], 1)

            def A2(s, t, u, j):
                neg_max(s, j, nmA, "nmA")
                if j == 3:
                    s.before("mTA", t)
                    two_parts(s, t, nmA[:].rearrange("p (h e) -> p e h", e=2), [nm2A[:, :, i, :] for i in range(2)],
                              "nmA", 4, "nm2A")

            def C4(s, t, u, j):
                neg_max(s, j, nmC, "nmC")
                if j == 1:
                    s.before("mTC", t)
                    two_parts(s, t, nmC[:], [nm2C[:, i, :] for i in range(2)], "nmC", 2, "nm2C")

            def A6(s, t, u, r):
                ps = s.read(s.part)[:].rearrange("p (g j c) -> p g j c", g=G0, c=SLOT)
                rl = rlA[:, r, :].rearrange("p (g j) -> p g j", g=G0).unsqueeze(3)
                chain(s, t, v.reciprocal(rl, ps[:, :, :, ONE0:ONE0 + 1]))
                v.tensor_tensor(oA[:, r * P:(r + 1) * P].rearrange("p (j g d) -> p g j d", j=4, g=G0), ps[:, :, :, 0:HD0],
                                rl.broadcast_to([P, G0, 4, HD0]), ALU.mult).then_inc(S["oA"], 1)
                if r == 1:
                    s.wait("oA", t, 2)
                    v.tensor_tensor(x1[u][:], oA[:], x0[u][:], ALU.add).then_inc(S["x1_done"], 1)

            def gated(ps, lo, n):
                return v.scalar_tensor_tensor(out=uB[:, lo:lo + n], in0=tB[:, lo:lo + n], scalar=1.0, in1=ps[:, 0:n],
                                              op0=ALU.add, op1=ALU.mult)

            def B2(s, t, u):
                s.wait("gate_exp", t)
                s.before("hB", t, 2)
                s.before("hTB", t, 3)

                def ch(ins):
                    chain(s, t, ins)

                ch(v.tensor_scalar(rt["den"][:], eB[:], 1.0, None, ALU.add))
                ch(v.reciprocal(rt["score"][:], rt["den"][:]))
                v.tensor_scalar(rt["half"][:], rt["score"][:], 0.5, None, ALU.mult).then_inc(S["score"], 1)
                if isinstance(t, int) and t == 0:
                    dve.wait_ge(S["bias_in"], 16)
                    dve.wait_ge(S["consts"], 2)
                ch(v.tensor_tensor(rt["v"][:], rt["score"][:], bias[:], ALU.add))
                other = rt["v"][:].unsqueeze(1).broadcast_to([P, E, E])
                own = rt["v"][:].unsqueeze(2).broadcast_to([P, E, E])
                chain(s, t, v.tensor_tensor(gt[:], other, own, ALU.is_gt), wait=False)
                ch(v.tensor_tensor(eq[:], other, own, ALU.is_equal))
                ch(v.tensor_tensor(eq[:], eq[:], before[:], ALU.mult))
                ch(v.tensor_tensor(gt[:], gt[:], eq[:], ALU.add))
                ch(v.tensor_reduce(rt["rank"][:], gt[:], FREE, ALU.add))
                ch(v.scalar_tensor_tensor(out=rt["sel"][:], in0=rt["rank"][:], scalar=1.5, in1=rt["score"][:],
                                          op0=ALU.is_lt, op1=ALU.mult))
                v.tensor_tensor(rt["c"][:], rt["sel"][:], rt["half"][:], ALU.mult).then_inc(S["route_c"], 1)
                ps = s.read(s.part)
                s.wait("tB", t, 3, 1)
                ch(gated(ps, E * HID, HID))
                v.scalar_tensor_tensor(out=hB[:, E * HID:], in0=uB[:, E * HID:], scalar=0.5, in1=ps[:, BANK:BANK + HID],
                                       op0=ALU.mult, op1=ALU.mult).then_inc(S["vB"], 1)

            def products(s, t, e0, k):
                ps = s.read(s.part)
                s.wait("tB", t, 3, k)
                chain(s, t, gated(ps, e0 * HID, BANK))
                v.tensor_tensor(vB[:, e0 * HID:e0 * HID + BANK], uB[:, e0 * HID:e0 * HID + BANK], ps[:, BANK:],
                                ALU.mult).then_inc(S["vB"], 1)

            def B3(s, t, u):
                products(s, t, 0, 2)

            def B4(s, t, u):
                products(s, t, 4, 3)

            def B6(s, t, u):
                ps = s.read(s.part)
                v.tensor_tensor(x2[u][:], ps[:, 0:D], x1[u][:], ALU.add).then_inc(S["x2_done"], 1)

            def C2(s, t, u, j):
                def heads(x):
                    return x.rearrange("p (h d) -> p h d", h=H1)

                ps = s.read(s.part)
                if j == 0:
                    s.wait("qC_hi", t)
                    v.tensor_tensor(heads(qrC[:]), heads(ps[:, 0:D]), qC[:, :, 0, :], ALU.subtract)\
                        .then_inc(S["qC_rest"], 1)
                else:
                    s.wait("VC", t)
                    v.tensor_tensor(heads(krC[:]), heads(ps[:, 0:D]), kC[:, :, 1, :], ALU.subtract)\
                        .then_inc(S["kC_rest"], 1)

            def C8(s, t, u):
                ps = s.read(s.part)[:].rearrange("p (h c) -> p h c", c=SLOT)
                s.before("oTC", t)
                v.reciprocal(rlC[:].unsqueeze(2), ps[:, :, ONE1:ONE1 + 1]).then_inc(S["rlC"], 1)
                s.wait("rlC", t)
                v.tensor_tensor(oC[:].rearrange("p (h d) -> p h d", d=HD1), ps[:, :, 0:HD1],
                                rlC[:].unsqueeze(2).broadcast_to([P, H1, HD1]), ALU.mult).then_inc(S["oC"], 1)

            def C10(s, t, u):
                ps = s.read(s.part)
                v.tensor_tensor(x3[u][:], ps[:, 0:D], x2[u][:], ALU.add).then_inc(S["x3_done"], 1)

            def D1(s, t, u):
                ps = s.read(s.part)
                v.tensor_copy(yT[:].rearrange("p c t -> p (c t)"), ps[:].bitcast(BF16)[:, 0:D]).then_inc(S["yT"], 1)

            def D2(s, t, u):
                ps = s.read(s.part)
                v.scalar_tensor_tensor(out=z[:], in0=ps[:], scalar=qs1[:, 1:2], in1=f1s[:], op0=ALU.mult, op1=ALU.mult)\
                    .then_inc(S["z"], 1)

            def D2b(s, t, u):
                s.wait("zz", t)
                v.scalar_tensor_tensor(out=inner[:], in0=zz[:], scalar=1.0, in1=z[:], op0=ALU.add, op1=ALU.mult)\
                    .then_inc(S["inner"], 1)

            def D2c(s, t, u):
                s.wait("th", t)
                chain(s, t, v.scalar_tensor_tensor(out=g2[:], in0=th[:], scalar=1.0, in1=z[:], op0=ALU.add, op1=ALU.mult))
                quantise(s, t, g2[:], 0.5, qs2[u])
                chain(s, t, v.tensor_scalar(g2[:], g2[:], qs2[u][:, 0:1], ROUND, ALU.mult, ALU.add))
                v.tensor_scalar(gq[:], g2[:], ROUND, 127.0, ALU.subtract, ALU.min).then_inc(S["gq"], 1)

            def D3(s, t, u):
                ps = s.read(s.part)
                v.tensor_copy(gT[:].rearrange("p k t -> p (k t)"), ps[:].bitcast(BF16)).then_inc(S["gT"], 1)

            def D4(s, t, u):
                s.before("x4_done", t)
                if not (isinstance(t, int) and t < 2):
                    dve.wait_ge(S[f"stored{u}"], (t - u) * 8)
                ps = s.read(s.part)
                v.scalar_tensor_tensor(out=y2[:], in0=ps[:, 0:D], scalar=qs2[u][:, 1:2], in1=f2s[:], op0=ALU.mult,
                                       op1=ALU.mult).then_inc(S["y2"], 1)
                s.wait("y2", t)
                v.tensor_tensor(x4[u][:], y2[:], x3[u][:], ALU.add).then_inc(S["x4_done"], 1)

            walk(dve, "vector", {
                "S1": S1, "S2": S2, "A0": A0, "B0": B0, "C0": C0, "D0": D0, "AX": AX, "BX": BX, "CX": CX,
                "DX": DX, "A1": A1, "A2": A2, "A6": A6, "B2": B2, "B3": B3, "B4": B4, "B6": B6, "C2": C2,
                "C4": C4, "C8": C8, "C10": C10, "D1": D1, "D2": D2, "D2b": D2b, "D2c": D2c, "D3": D3, "D4": D4,
            }, chain)


def kernel(**inputs):
    import concourse.bacc as bacc
    from concourse.bass_utils import run_bass_kernel_spmd

    get = {k: np.asarray(v) for k, v in inputs.items()}
    x = get["x"]
    tiles = x.shape[0]

    def laid(v, *shape):
        return np.ascontiguousarray(v).reshape(shape)

    arrays = {
        "x": laid(x, tiles, P, D),
        "ctx": laid(get["ctx_512"], tiles, P, L),
        "ctxT": laid(get["ctx_512"].transpose(0, 2, 1), tiles, L, P),
        "bias": laid(get["L0_ffn_expert_bias"], E),
        "gateT": laid(get["L0_ffn_gate_w"].T, DC, P, E),
        "w1T": laid(get["L0_ffn_w1"].transpose(2, 0, 1), DC, P, E * HID),
        "w3T": laid(get["L0_ffn_w3"].transpose(2, 0, 1), DC, P, E * HID),
        "w2T": laid(get["L0_ffn_w2"].transpose(0, 2, 1), E, HID, D),
        "sw1T": laid(get["L0_ffn_sw1"].T, DC, P, HID),
        "sw3T": laid(get["L0_ffn_sw3"].T, DC, P, HID),
        "sw2T": laid(get["L0_ffn_sw2"].T, HID, D),
        "WqT": laid(get["L1_xattn_Wq"].T, DC, P, D),
        "WkvT": laid(get["L1_xattn_Wkv_expand"].T, L, 2 * D),
        "WoutT": laid(get["L1_xattn_Wout"].T, DC, P, D),
        "f1T": laid(get["L1_ffn_w1"].T, DC, P, HF),
        "f2T": laid(get["L1_ffn_w2"].T, FC, P, D),
    }
    nc = bacc.Bacc("TRN2", target_bir_lowering=False, num_devices=1)
    a = {k: nc.dram_tensor(f"in_{k}", v.shape, F32, kind="ExternalInput").ap() for k, v in arrays.items()}
    out = nc.dram_tensor("out", (tiles, P, D), F32, kind="ExternalOutput").ap()
    build(nc, a, out, tiles)
    r = run_bass_kernel_spmd(nc, [{f"in_{k}": v for k, v in arrays.items()}], core_ids=[0])
    return r.results[0]["out"]
```
